# Optimizing a Trainium2 kernel written in Bass

```python
import numpy as np
import jax
import jax.numpy as jnp

def _softmax(x, axis=-1):
    return jax.nn.softmax(x, axis=axis)

def _gelu(x):
    return jax.nn.gelu(x, approximate=True)

def _silu(x):
    return jax.nn.silu(x)

def _sigmoid(x):
    return jax.nn.sigmoid(x)

def _layernorm(x, axis=-1, eps=1e-05):
    m = jnp.mean(x, axis=axis, keepdims=True)
    v = jnp.var(x, axis=axis, keepdims=True)
    return (x - m) / jnp.sqrt(v + eps)

def _scatter_add(tgt, idx, src, axis=0):
    return tgt.at[idx].add(src)

def _segment_sum(src, seg, n):
    return jax.ops.segment_sum(src, seg, n)
kernel_name = 'mk_xattn_ffn_d2_seqx_r4_59361c'

def setup_inputs(seed: int=0):
    np.random.seed(seed)
    _w = jnp.asarray

    def _rec_inputs():
        import jax
        import jax.numpy as jnp
        _rk = jax.random.key(seed)
        x = -0.000125 + 0.9999 * jax.random.normal(jax.random.fold_in(_rk, 1), (8, 256, 1024), jnp.float32)
        _lenS = 256 - jax.random.randint(jax.random.fold_in(_rk, 7), (8,), 0, max(1, 256 // 4) + 1, jnp.int32)
        _lenS2 = 256 - jax.random.randint(jax.random.fold_in(_rk, 8), (8,), 0, max(1, 256 // 4) + 1, jnp.int32)
        _ctx_4096P = jax.random.normal(jax.random.fold_in(_rk, 11), (8, 16, 1024), jnp.float32)
        _ctx_4096c = jax.random.dirichlet(jax.random.fold_in(_rk, 511), 0.3 * jnp.ones((16,), jnp.float32), (8, 256))
        _ctx_4096t = jnp.einsum('bsk,bkd->bsd', _ctx_4096c, _ctx_4096P)
        _ctx_4096t = _ctx_4096t * jax.lax.rsqrt(jnp.mean(jnp.square(_ctx_4096t)) + 1e-12) * 0.953939
        ctx_4096 = -1.52775e-05 + 0.999936 * (_ctx_4096t + 0.3 * jax.random.normal(jax.random.fold_in(_rk, 611), (8, 256, 1024), jnp.float32))
        return (x, ctx_4096)
    x, ctx_4096 = _rec_inputs()

    def _L0_xattn_setup():
        import jax, jax.numpy as jnp
        import numpy as np
        import math
        EPS = 1e-05
        LAMBDA = 0.6

        def _crucial_k(C):
            f = math.floor(LAMBDA * C)
            return f + f % 2

        def _conv1d(y, w):
            return jax.lax.conv_general_dilated(y, w, window_strides=(1,), padding=((3, 3),), dimension_numbers=('NCH', 'OIH', 'NCH'))

        def _norm_active(z, gamma, beta):
            mu = jnp.mean(z, axis=(0, 2), keepdims=True)
            var = jnp.mean((z - mu) ** 2, axis=(0, 2), keepdims=True)
            zn = (z - mu) * jax.lax.rsqrt(var + EPS)
            zn = zn * gamma.reshape(1, -1, 1) + beta.reshape(1, -1, 1)
            return jax.nn.sigmoid(jax.nn.relu(zn))
        key = jax.random.key(seed)
        k1, k2, k3 = jax.random.split(key, 3)
        B, C, L = (32, 64, 1024)
        x = jax.random.normal(k1, (B, C, L), dtype=jnp.float32)
        channel_map = jax.random.normal(k2, (B, C, L), dtype=jnp.float32)
        fan_in = 2 * 7
        bound = 1.0 / math.sqrt(fan_in)
        conv_w = jax.random.uniform(k3, (1, 2, 7), jnp.float32, -bound, bound)
        bn_gamma = jnp.ones((1,), jnp.float32)
        bn_beta = jnp.zeros((1,), jnp.float32)
        return {'x': x, 'channel_map': channel_map, 'conv_w': conv_w, 'bn_gamma': bn_gamma, 'bn_beta': bn_beta}
    _L0_xattn_all = _L0_xattn_setup()
    _L0_xattn_in = {k: v for k, v in _L0_xattn_all.items() if k in ('conv_w', 'bn_gamma', 'bn_beta')}
    del _L0_xattn_all

    def _L0_ffn_setup():
        import jax, jax.numpy as jnp
        import numpy as np
        ALPHA = 32
        R = 16
        SCALING = ALPHA / R
        key = jax.random.key(seed)
        k1, k2, k3, k4 = jax.random.split(key, 4)
        B_, S, D = (4, 512, 1024)
        H, r, O = (8, R, 1024)
        x = jax.random.normal(k1, (B_, S, D), dtype=jnp.float32)
        A = jax.random.normal(k2, (H, r, D), dtype=jnp.float32) * 0.02
        Bm = jax.random.normal(k3, (H, O, r), dtype=jnp.float32) * 0.02
        Wr = jax.random.normal(k4, (H, D), dtype=jnp.float32) * 0.02
        br = jnp.zeros((H,), dtype=jnp.float32)
        return {'x': x, 'A': A, 'B': Bm, 'Wr': Wr, 'br': br}
    _L0_ffn_all = _L0_ffn_setup()
    _L0_ffn_in = {k: v for k, v in _L0_ffn_all.items() if k in ('A', 'B', 'Wr', 'br')}
    del _L0_ffn_all

    def _L1_xattn_setup():
        import jax, jax.numpy as jnp
        import numpy as np
        key = jax.random.key(seed)
        k1, k2 = jax.random.split(key)
        B, Lq, Lk, D = (16, 256, 512, 1024)
        query = jax.random.normal(k1, (B, Lq, D), dtype=jnp.float32)
        key_t = jax.random.normal(k2, (B, Lk, D), dtype=jnp.float32)
        return {'query': query, 'key': key_t}
    _L1_xattn_all = _L1_xattn_setup()
    _L1_xattn_in = {k: v for k, v in _L1_xattn_all.items() if k in ()}
    del _L1_xattn_all

    def _L1_ffn_setup():
        import jax, jax.numpy as jnp
        import numpy as np
        D_IN = 1024
        D_OUT = 1024
        RANK = 16
        NUM_EXPERTS = 8
        TOP_K = 2
        SCALING = 32.0 / RANK
        key = jax.random.key(seed)
        ks = jax.random.split(key, 6)
        x = jax.random.normal(ks[0], (4, 512, D_IN), dtype=jnp.float32)
        W_base = jax.random.normal(ks[1], (D_OUT, D_IN), dtype=jnp.float32) * (1.0 / np.sqrt(D_IN))
        b_base = jax.random.normal(ks[2], (D_OUT,), dtype=jnp.float32) * 0.01
        W_router = jax.random.normal(ks[3], (NUM_EXPERTS, D_IN), dtype=jnp.float32) * 0.01
        A_stack = jax.random.uniform(ks[4], (NUM_EXPERTS, RANK, D_IN), dtype=jnp.float32, minval=-1.0, maxval=1.0) * (1.0 / np.sqrt(D_IN))
        B_stack = jax.random.normal(ks[5], (NUM_EXPERTS, D_OUT, RANK), dtype=jnp.float32) * 0.02
        return {'x': x, 'W_base': W_base, 'b_base': b_base, 'W_router': W_router, 'A_stack': A_stack, 'B_stack': B_stack}
    _L1_ffn_all = _L1_ffn_setup()
    _L1_ffn_in = {k: v for k, v in _L1_ffn_all.items() if k in ('W_base', 'b_base', 'W_router', 'A_stack', 'B_stack')}
    del _L1_ffn_all
    return {'x': x, 'ctx_4096': ctx_4096, 'L0_xattn_conv_w': _L0_xattn_in['conv_w'], 'L0_xattn_bn_gamma': _L0_xattn_in['bn_gamma'], 'L0_xattn_bn_beta': _L0_xattn_in['bn_beta'], 'L0_ffn_A': _L0_ffn_in['A'], 'L0_ffn_B': _L0_ffn_in['B'], 'L0_ffn_Wr': _L0_ffn_in['Wr'], 'L0_ffn_br': _L0_ffn_in['br'], 'L1_ffn_W_base': _L1_ffn_in['W_base'], 'L1_ffn_b_base': _L1_ffn_in['b_base'], 'L1_ffn_W_router': _L1_ffn_in['W_router'], 'L1_ffn_A_stack': _L1_ffn_in['A_stack'], 'L1_ffn_B_stack': _L1_ffn_in['B_stack']}

def reference(x, ctx_4096, L0_xattn_conv_w, L0_xattn_bn_gamma, L0_xattn_bn_beta, L0_ffn_A, L0_ffn_B, L0_ffn_Wr, L0_ffn_br, L1_ffn_W_base, L1_ffn_b_base, L1_ffn_W_router, L1_ffn_A_stack, L1_ffn_B_stack):
    import jax
    import jax.numpy as jnp

    def _L0_xattn_ref(x, channel_map, conv_w, bn_gamma, bn_beta):
        import jax, jax.numpy as jnp
        import numpy as np
        import math
        EPS = 1e-05
        LAMBDA = 0.6

        def _crucial_k(C):
            f = math.floor(LAMBDA * C)
            return f + f % 2

        def _conv1d(y, w):
            return jax.lax.conv_general_dilated(y, w, window_strides=(1,), padding=((3, 3),), dimension_numbers=('NCH', 'OIH', 'NCH'))

        def _norm_active(z, gamma, beta):
            mu = jnp.mean(z, axis=(0, 2), keepdims=True)
            var = jnp.mean((z - mu) ** 2, axis=(0, 2), keepdims=True)
            zn = (z - mu) * jax.lax.rsqrt(var + EPS)
            zn = zn * gamma.reshape(1, -1, 1) + beta.reshape(1, -1, 1)
            return jax.nn.sigmoid(jax.nn.relu(zn))
        B, C, L = x.shape
        k = _crucial_k(C)
        cm = jnp.moveaxis(channel_map, 1, 2)
        _, topk_idx = jax.lax.top_k(cm, k)
        b_idx = jnp.arange(B)[:, None, None]
        l_idx = jnp.arange(L)[None, :, None]
        mask = jnp.zeros((B, L, C), x.dtype).at[b_idx, l_idx, topk_idx].set(1.0)
        crucial_channels = jnp.moveaxis(mask, 2, 1)
        subcrucial_channels = 1.0 - crucial_channels
        crucial_features = crucial_channels * x
        subcrucial_features = subcrucial_channels * x
        c_max = jnp.max(crucial_features, axis=1, keepdims=True)
        c_avg = jnp.mean(crucial_features, axis=1, keepdims=True) * (C / k)
        s_max = jnp.max(subcrucial_features, axis=1, keepdims=True)
        s_avg = jnp.mean(subcrucial_features, axis=1, keepdims=True) * (C / (C - k))
        crucial_x = jnp.concatenate([c_max, c_avg], axis=1)
        subcrucial_x = jnp.concatenate([s_max, s_avg], axis=1)
        A_S1 = _norm_active(_conv1d(crucial_x, conv_w), bn_gamma, bn_beta)
        A_S2 = _norm_active(_conv1d(subcrucial_x, conv_w), bn_gamma, bn_beta)
        return crucial_features * A_S1 + subcrucial_features * A_S2

    def _L0_ffn_ref(x, A, B, Wr, br):
        import jax, jax.numpy as jnp
        import numpy as np
        ALPHA = 32
        R = 16
        SCALING = ALPHA / R
        H = A.shape[0]
        router_logits = jnp.einsum('bsd,hd->bsh', x, Wr) + br
        scores = H * jax.nn.softmax(router_logits, axis=-1)
        low = jnp.einsum('bsd,hrd->bshr', x, A)
        out = jnp.einsum('bshr,hor,bsh->bso', low, B, scores)
        return SCALING * out

    def _L1_xattn_ref(query, key):
        import jax, jax.numpy as jnp
        import numpy as np
        a = jnp.einsum('bqd,bkd->bqk', query, key)
        e = jax.nn.softmax(a, axis=-1)
        c = jnp.einsum('bqk,bkd->bqd', e, key)
        return c

    def _L1_ffn_ref(x, W_base, b_base, W_router, A_stack, B_stack):
        import jax, jax.numpy as jnp
        import numpy as np
        D_IN = 1024
        D_OUT = 1024
        RANK = 16
        NUM_EXPERTS = 8
        TOP_K = 2
        SCALING = 32.0 / RANK
        orig_shape = x.shape
        xf = x.reshape(-1, D_IN)
        logits = xf @ W_router.T
        probs = jax.nn.softmax(logits, axis=-1)
        topk_p, topk_i = jax.lax.top_k(probs, TOP_K)
        topk_p = topk_p / jnp.sum(topk_p, axis=-1, keepdims=True)
        combine = jnp.sum(jax.nn.one_hot(topk_i, NUM_EXPERTS, dtype=xf.dtype) * topk_p[..., None], axis=1)
        h = jnp.einsum('nd,erd->ner', xf, A_stack)
        h = h * combine[..., None]
        lora_out = jnp.einsum('ner,eor->no', h, B_stack) * SCALING
        base_out = xf @ W_base.T + b_base
        out = base_out + lora_out
        return out.reshape(orig_shape[:-1] + (D_OUT,))
    x = x + _L0_xattn_ref(_layernorm(x, axis=-1), ctx_4096, L0_xattn_conv_w, L0_xattn_bn_gamma, L0_xattn_bn_beta)
    x = x + _L0_ffn_ref(_layernorm(x, axis=-1), L0_ffn_A, L0_ffn_B, L0_ffn_Wr, L0_ffn_br)
    x = x + _L1_xattn_ref(_layernorm(x, axis=-1), ctx_4096)
    x = x + _L1_ffn_ref(_layernorm(x, axis=-1), L1_ffn_W_base, L1_ffn_b_base, L1_ffn_W_router, L1_ffn_A_stack, L1_ffn_B_stack)
    return x

_drawn_inputs = setup_inputs


def setup_inputs(seed=0):
    import zlib

    import numpy as np

    out = dict(_drawn_inputs(seed))
    spreads = {'L0_ffn_br': (0.0, 0.1)}
    factors = {'L1_ffn_b_base': 8.0}
    for name, (base, spread) in spreads.items():
        noise = np.random.default_rng([zlib.crc32(name.encode()), seed]).standard_normal(out[name].shape)
        drawn = base * np.exp(spread * noise) if base else spread * noise
        out[name] = jnp.asarray(drawn.astype(out[name].dtype))
    for name, factor in factors.items():
        out[name] = (out[name] * factor).astype(out[name].dtype)
    return out
```

```python
from contextlib import ExitStack

import concourse.bass as bass
from concourse import mybir

ALU = mybir.AluOpType
ACT = mybir.ActivationFunctionType
AX_X = mybir.AxisListType.X
F32 = mybir.dt.float32
F16 = mybir.dt.float16
BF16 = mybir.dt.bfloat16

P = 128
B = 8
C = 256
D = 1024
CH = C // P
DC = D // P
NT = B * CH
HALF = 512
TOP = 154
TAPS = 7
H = 8
R = 16
HR = H * R
WA = HR + H
EPS_LN = 1e-5
EPS_BN = 1e-5
WS = 64.0
LORA = 2.0
TAKEN = -3.4028234663852886e38


def rounds(eng, n):
    yield 0
    if n > 1:
        with eng.Fori(1, n) as i:
            yield i


def after(tile):
    pair, slot = tile
    return (pair, 1) if slot == 0 else (pair + 1, 0)


def count(tile):
    return tile[0] + 1


def build_kernel(nc, x, ctx_in, conv_w, bn_gamma, bn_beta, A0, B0, Wr0, br0, W_base, b_base, Wr1, A1, B1, out):
    stack = ExitStack()
    with stack:
        def sb(name, shape, dt=F32, scope=stack):
            return scope.enter_context(nc.sbuf_tensor(name, shape, dt))

        def ps(name, shape, scope, dt=F32):
            return scope.enter_context(nc.psum_tensor(name, shape, dt))

        def sem(name):
            return stack.enter_context(nc.semaphore(name))

        def sems(name, n=2):
            return [sem(f"{name}{i}") for i in range(n)]

        base_hi = sb("base_hi", [P, DC, D], F16)
        base_lo = sb("base_lo", [P, DC, D], F16)
        down_hi = [sb(f"down_hi{i}", [P, DC, WA], F16) for i in range(2)]
        down_lo = [sb(f"down_lo{i}", [P, DC, WA], F16) for i in range(2)]
        up_hi = [sb(f"up_hi{i}", [P, D], F16) for i in range(2)]
        up_lo = [sb(f"up_lo{i}", [P, D], F16) for i in range(2)]
        ident = sb("ident", [P, P])
        ones = sb("ones", [P, P])
        minus_half = sb("minus_half", [P, 2])
        br_bc = sb("br_bc", [P, H])
        bias_bc = sb("bias_bc", [P, D])

        const_ready = sem("const_ready")
        small_in = sem("small_in")

        shared = sb("shared", [P, 4 * CH * 2 * D], F16)
        mask = shared[:, :].bitcast(BF16).rearrange("p (b l c) -> p b l c", b=B, l=DC)
        mean_x = sb("mean_x", [P, NT])
        rstd_x = sb("rstd_x", [P, NT])
        coef = sb("coef", [P, 2, B * DC])
        dcoef = sb("dcoef", [P, B * DC])
        phase_channels(nc, sb, ps, sem, sems, locals())
        resid = sb("resid", [P, NT, D])
        phase_apply(nc, sb, ps, sem, sems, locals())
        norm = Norm(nc, sb, ps, sems, resid, ident, minus_half, const_ready)
        phase_lora(nc, sb, ps, sem, sems, locals())
        phase_attention(nc, sb, ps, sem, sems, locals())
        phase_ffn(nc, sb, ps, sem, sems, locals())


def phase_channels(nc, sb, ps, sem, sems, env):
    x, ctx_in, W_base = env["x"], env["ctx_in"], env["W_base"]
    ident, ones, minus_half = env["ident"], env["ones"], env["minus_half"]
    mask, mean_x, rstd_x, coef, dcoef = (env[k] for k in ("mask", "mean_x", "rstd_x", "coef", "dcoef"))
    const_ready, small_in = env["const_ready"], env["small_in"]
    scope = ExitStack()
    with scope:
        w_in = [sb(f"w_in{s}", [P, D], F32, scope) for s in range(2)]
        x_in = [sb(f"x_in{h}", [P, D], F32, scope) for h in range(CH)]
        c_in = [sb(f"c_in{h}", [P, D], F32, scope) for h in range(CH)]
        xn = [sb(f"xn{h}", [P, D], F32, scope) for h in range(CH)]
        xt = sb("xt", [P, DC, C], F32, scope)
        keys = sb("keys", [P, DC, C], F32, scope)
        cruc = sb("cruc", [P, DC, C], F32, scope)
        subc = sb("subc", [P, DC, C], F32, scope)
        work = sb("work", [P, C], F32, scope)
        top8 = sb("top8", [P, 8], F32, scope)
        stats = sb("stats", [P, CH, 2, 6], F32, scope)
        mv = sb("mv", [P, CH, 2], F32, scope)
        ve = sb("ve", [P, CH], F32, scope)
        taken = sb("taken", [P, DC, C], BF16, scope)
        largest = sb("largest", [P, 2, DC], F32, scope)
        maps = sb("maps", [P, 2, 2, B, DC + 2], F32, scope)
        wide = sb("wide", [P, 384 + TAPS - 1], F32, scope)
        band = [sb(f"band{c}", [P, 384], F32, scope) for c in range(2)]
        taps = sb("taps", [P, 2 * TAPS], F32, scope)
        bn = sb("bn", [P, 2], F32, scope)
        zc = sb("zc", [P, 2, B * DC], F32, scope)
        zq = sb("zq", [P, 2, B * DC], F32, scope)
        zs = sb("zs", [P, 2], F32, scope)
        zm = sb("zm", [P, 2], F32, scope)
        zv = sb("zv", [P, 2], F32, scope)
        zr = sb("zr", [P, 2], F32, scope)
        zg = sb("zg", [P, 2], F32, scope)
        bank = [ps(f"bank{i}", [P, 2 * HALF], scope) for i in range(4)]
        x_ps, c_ps = bank[0:2], bank[2:4]

        w_loaded, w_turned, w_split, w_hi = (sems(n) for n in ("w_loaded", "w_turned", "w_split", "w_hi"))
        x_loaded, c_loaded, x_normed = (sems(n) for n in ("x_loaded", "c_loaded", "x_normed"))
        x_stats, x_rstd, x_var = sem("x_stats"), sem("x_rstd"), sem("x_var")
        xt_turned, keys_turned, xt_copied, keys_copied = (
            sem(n) for n in ("xt_turned", "keys_turned", "xt_copied", "keys_copied"))
        chain, batch_split, sums_done = (sem(n) for n in ("chain", "batch_split", "sums_done"))
        tail, maps_scaled, z_done, z_sums, z_var, z_rstd, z_act_in, z_act = (
            sem(n) for n in ("tail", "maps_scaled", "z_done", "z_sums", "z_var", "z_rstd", "z_act_in", "z_act"))

        down_hi, down_lo, up_hi, up_lo = (env[k] for k in ("down_hi", "down_lo", "up_hi", "up_lo"))
        NW = DC

        def into_base(o):
            return lambda part, half: env["base_" + part][:, 4 * half:4 * half + 4, bass.ts(o, P)]

        def into_down(i, c0, c1):
            d = {"hi": down_hi[i], "lo": down_lo[i]}
            return lambda part, half: d[part][:, 4 * half:4 * half + 4, c0:c1]

        def into_up(i):
            d = {"hi": up_hi[i], "lo": up_lo[i]}
            return lambda part, half: d[part][:, half * HALF:(half + 1) * HALF].rearrange("p (c n) -> p c n", c=4)

        few = []
        for i, (a, w, bm) in enumerate(((env["A0"], env["Wr0"], env["B0"]), (env["A1"], env["Wr1"], env["B1"]))):
            few.append((a.rearrange("h r d -> (h r) d"), P, P, into_down(i, 0, HR), None))
            few.append((w, H, H, into_down(i, HR, WA), None))
            few.append((bm.rearrange("h (c p) r -> p c h r", p=P), P, P, into_up(i), "up"))

        W_ITEMS = NW + len(few)
        arrived, per_slot = [], [16 * NW // 2] * 2
        for n, item in enumerate(few):
            per_slot[(NW + n) % 2] += 16 * (DC if item[4] == "up" else 1)
            arrived.append(per_slot[(NW + n) % 2])

        block = scope.enter_context(nc.Block())

        @block.sync
        def _(sp):
            sp.dma_start(env["br_bc"][:, :], env["br0"].partition_broadcast(P)).then_inc(small_in, 16)
            sp.dma_start(env["bias_bc"][:, :], env["b_base"].partition_broadcast(P)).then_inc(small_in, 16)
            sp.dma_start(taps[:, :], env["conv_w"].rearrange("a c t -> (a c t)").partition_broadcast(P)).then_inc(small_in, 16)
            sp.dma_start(bn[:, 0:1], env["bn_gamma"].partition_broadcast(P)).then_inc(small_in, 16)
            sp.dma_start(bn[:, 1:2], env["bn_beta"].partition_broadcast(P)).then_inc(small_in, 16)
            for p in rounds(sp, NW // 2):
                for s in range(2):
                    sp.wait_ge(w_turned[s], p)
                    sp.dma_start(w_in[s][:, :], W_base[bass.ts(2 * p + s, P), :]).then_inc(w_loaded[s], 16)
            for n, (src, rows, _, _, kind) in enumerate(few):
                s, p = (NW + n) % 2, (NW + n) // 2
                sp.wait_ge(w_turned[s], p)
                if kind == "up":
                    for c in range(DC):
                        sp.dma_start(w_in[s][:, c * P:(c + 1) * P].rearrange("p (h r) -> p h r", h=H),
                                     src[:, c]).then_inc(w_loaded[s], 16)
                else:
                    sp.dma_start(w_in[s][0:rows, :], src).then_inc(w_loaded[s], 16)
            for b in rounds(sp, B):
                for h in range(CH):
                    sp.wait_ge(x_normed[h], b)
                    sp.dma_start(x_in[h][:, :], x[b, h * P:(h + 1) * P, :]).then_inc(x_loaded[h], 16)
                    sp.wait_ge(keys_turned, 4 * b)
                    sp.dma_start(c_in[h][:, :], ctx_in[b, h * P:(h + 1) * P, :]).then_inc(c_loaded[h], 16)

        @block.gpsimd
        def _(pool):
            pool.memset(ident[:, :], 0.0).then_inc(const_ready, 1)
            pool.memset(wide[:, :], 0.0).then_inc(const_ready, 1)
            pool.memset(ones[:, :], 1.0).then_inc(const_ready, 1)
            pool.memset(minus_half[:, :], -0.5).then_inc(const_ready, 1)
            pool.wait_ge(const_ready, 2)
            pool.affine_select(out=ident[:, :], in_=ident[:, :], compare_op=ALU.not_equal, fill=1.0, base=0,
                               pattern=[[-1, P]], channel_multiplier=1).then_inc(const_ready, 1)
            pool.affine_select(out=wide[:, :], in_=wide[:, :], compare_op=ALU.not_equal, fill=1.0,
                               base=131, pattern=[[-1, 384 + TAPS - 1]], channel_multiplier=1).then_inc(const_ready, 1)
            pool.wait_ge(const_ready, 6)
            for b in rounds(pool, B):
                wait_alone(pool, const_ready, (x_stats, b + 1))
                pool.tensor_scalar(ve[:, :], mv[:, :, 1], EPS_LN, None, ALU.add).then_inc(x_var, 1)
                wait_alone(pool, const_ready, (x_var, b + 1))
                pool.tensor_tensor(rstd_x[:, bass.ts(b, CH)], ve[:, :], minus_half[:, :], ALU.pow).then_inc(x_rstd, 1)
            pool.wait_ge(z_var, 1)
            pool.tensor_tensor(zr[:, :], zv[:, :], minus_half[:, :], ALU.pow).then_inc(z_rstd, 1)

        @block.scalar
        def _(act):
            def hi_parts(dest, s, cols):
                for half in range(2):
                    src = bank[s][:, half * HALF:(half + 1) * HALF].rearrange("p (c n) -> p c n", c=4)[:, :, 0:cols]
                    last = act.activation(dest("hi", half), src, ACT.Copy, scale=WS)
                last.then_inc(w_hi[s], 1)

            for p in rounds(act, NW // 2):
                for s in range(2):
                    act.wait_ge(w_turned[s], p + 1)
                    hi_parts(into_base(2 * p + s), s, P)
            for n, (_, _, cols, dest, _) in enumerate(few):
                s, p = (NW + n) % 2, (NW + n) // 2
                act.wait_ge(w_turned[s], p + 1)
                hi_parts(dest, s, cols)
            for b in rounds(act, B):
                act.wait_ge(batch_split, b)
                for g in range(4):
                    act.wait_ge(xt_turned, 4 * b + g + 1)
                    act.activation(xt[:, 2 * g:2 * g + 2, :],
                                   x_ps[g // 2][:, bass.ts(g % 2, HALF)].rearrange("p (u c) -> p u c", u=2),
                                   ACT.Copy).then_inc(xt_copied, 1)
                    act.wait_ge(keys_turned, 4 * b + g + 1)
                    act.activation(keys[:, 2 * g:2 * g + 2, :],
                                   c_ps[g // 2][:, bass.ts(g % 2, HALF)].rearrange("p (u c) -> p u c", u=2),
                                   ACT.Copy).then_inc(keys_copied, 1)
                act.wait_ge(batch_split, b + 1)
                for c in range(DC):
                    act.activation(cruc[:, c, :], cruc[:, c, :], ACT.Copy, accum_out=maps[:, 0, 1, b, c + 1:c + 2])
                    last = act.activation(subc[:, c, :], subc[:, c, :], ACT.Copy,
                                          accum_out=maps[:, 1, 1, b, c + 1:c + 2])
                last.then_inc(sums_done, 1)
            act.wait_ge(z_act_in, 1)
            act.activation(coef[:, :, :], zc[:, :, :], ACT.Sigmoid).then_inc(z_act, 1)

        @block.tensor
        def _(pe):
            pe.wait_ge(const_ready, 6)

            def turn_weights(s, rows, cols, done, loaded):
                pe.wait_ge(w_loaded[s], loaded)
                pe.wait_ge(w_hi[s], done)
                pe.wait_ge(w_split[s], done)
                for c in range(DC):
                    last = pe.transpose(bank[s][:, c * P:c * P + cols], w_in[s][0:rows, c * P:(c + 1) * P],
                                        ident[0:rows, 0:rows])
                last.then_inc(w_turned[s], 1)

            for p in rounds(pe, NW // 2):
                for s in range(2):
                    turn_weights(s, P, P, p, 16 * p + 16)
            for n, (_, rows, cols, _, _) in enumerate(few):
                s, p = (NW + n) % 2, (NW + n) // 2
                turn_weights(s, rows, cols, p, arrived[n])
            for s in range(2):
                pe.wait_ge(w_hi[s], W_ITEMS // 2)
                pe.wait_ge(w_split[s], W_ITEMS // 2)
            for b in rounds(pe, B):
                for h in range(CH):
                    pe.wait_ge(x_normed[h], b + 1)
                    pe.wait_ge(c_loaded[h], 16 * b + 16)
                pe.wait_ge(xt_copied, 4 * b)
                pe.wait_ge(keys_copied, 4 * b)
                for g in range(4):
                    for dst, src, turned in ((x_ps, xn, xt_turned), (c_ps, c_in, keys_turned)):
                        for u in range(2):
                            for h in range(CH):
                                at = (g % 2) * HALF + u * C + h * P
                                c = 2 * g + u
                                last = pe.transpose(dst[g // 2][:, at:at + P], src[h][:, c * P:(c + 1) * P],
                                                    ident[:, :])
                        last.then_inc(turned, 1)
            pe.wait_ge(xt_copied, 4 * B)
            pe.wait_ge(sums_done, B)
            pe.wait_ge(maps_scaled, 2)
            n = 0
            for ch in range(2):
                for shift, at in ((0, 256), (1, 128), (2, 0)):
                    n += 1
                    last = pe.matmul(bank[0][:, 0:2 * B * DC].rearrange("p (k b c) -> p k b c", k=2, b=B),
                                     band[ch][:, at:at + P], maps[:, :, ch, :, shift:shift + DC],
                                     start=(n == 1), stop=(n == 6))
            last.then_inc(z_done, 1)
            for n in range(2):
                pe.wait_ge(z_sums, n + 1)
                pe.matmul(bank[1][:, 2 * n:2 * n + 2], ones[:, :], zs[:, :], start=True, stop=True).then_inc(z_done, 1)

        @block.vector
        def _(dve):
            def lo_parts(dest, s, cols):
                for half in range(2):
                    src = bank[s][:, half * HALF:(half + 1) * HALF].rearrange("p (c n) -> p c n", c=4)[:, :, 0:cols]
                    last = dve.scalar_tensor_tensor(dest("lo", half), src, WS, dest("hi", half), ALU.mult, ALU.subtract)
                last.then_inc(w_split[s], 1)

            for p in rounds(dve, NW // 2):
                for s in range(2):
                    dve.wait_ge(w_hi[s], p + 1)
                    lo_parts(into_base(2 * p + s), s, P)
            for n, (_, _, cols, dest, _) in enumerate(few):
                s, p = (NW + n) % 2, (NW + n) // 2
                dve.wait_ge(w_hi[s], p + 1)
                lo_parts(dest, s, cols)

            dve.memset(maps[:, :, :, :, :].rearrange("p a b c d -> p (a b c d)"), 0.0).then_inc(tail, 1)
            dve.wait_ge(small_in, 80)
            dve.wait_ge(const_ready, 6)
            dve.wait_ge(tail, 1)
            for ch in range(2):
                for t in range(TAPS):
                    w = taps[:, ch * TAPS + t:ch * TAPS + t + 1]
                    if t == 0:
                        ins = dve.tensor_scalar(band[ch][:, :], wide[:, 0:384], w, None, ALU.mult)
                    else:
                        ins = dve.scalar_tensor_tensor(band[ch][:, :], wide[:, t:t + 384], w, band[ch][:, :],
                                                       ALU.mult, ALU.add)
                    ins.then_inc(chain, 1)
                    dve.wait_ge(chain, ch * TAPS + t + 1)
            LEAD = 2 * TAPS
            n_rounds = (TOP + 7) // 8
            PER_BATCH = 5 + DC * (2 * n_rounds + 4)
            left = TOP - 8 * (n_rounds - 1)
            for b in rounds(dve, B):
                n_links = 0

                def link(ins):
                    nonlocal n_links
                    n_links += 1
                    ins.then_inc(chain, 1)
                    wait_alone(dve, const_ready, (chain, LEAD + b * PER_BATCH + n_links))

                for h in range(CH):
                    dve.wait_ge(x_loaded[h], 16 * b + 16)
                    for k in range(2):
                        last = dve.bn_stats(stats[:, h, k, :], x_in[h][:, k * HALF:(k + 1) * HALF])
                dve.wait_ge(x_rstd, b)
                link(last)
                for h in range(CH):
                    last = dve.bn_aggr(mv[:, h, :], stats[:, h, :, :])
                last.then_inc(x_stats, 1)
                dve.wait_ge(x_stats, b + 1)
                link(dve.tensor_copy(mean_x[:, bass.ts(b, CH)], mv[:, :, 0]))
                dve.wait_ge(x_rstd, b + 1)
                dve.wait_ge(xt_turned, 4 * b)
                for h in range(CH):
                    dve.tensor_scalar(xn[h][:, :], x_in[h][:, :], mv[:, h, 0:1], rstd_x[:, bass.ds(CH * b + h, 1)],
                                      ALU.subtract, ALU.mult).then_inc(x_normed[h], 1)
                wait_alone(dve, const_ready, (xt_copied, 4 * b + 4), (keys_copied, 4 * b + 4), (sums_done, b))
                for c in range(DC):
                    for r in range(n_rounds):
                        src = keys[:, c, :] if r == 0 else work[:, :]
                        link(dve.max(top8[:, :], src))
                        if r == n_rounds - 1 and left < 8:
                            link(dve.memset(top8[:, left:8], TAKEN))
                        link(dve.match_replace(work[:, :], top8[:, :], src, TAKEN))
                    link(dve.tensor_tensor(taken[:, c, :], work[:, :], keys[:, c, :], ALU.not_equal))
                    link(dve.tensor_tensor_reduce(out=cruc[:, c, :], in0=taken[:, c, :], in1=xt[:, c, :], scale=1.0,
                                                  scalar=TAKEN, op0=ALU.mult, op1=ALU.max,
                                                  accum_out=largest[:, 0, c:c + 1]))
                    link(dve.tensor_tensor_reduce(out=subc[:, c, :], in0=xt[:, c, :], in1=cruc[:, c, :], scale=1.0,
                                                  scalar=TAKEN, op0=ALU.subtract, op1=ALU.max,
                                                  accum_out=largest[:, 1, c:c + 1]))
                dve.sem_inc(batch_split, 1)
                link(dve.tensor_copy(mask[:, b, :, :], taken[:, :, :]))
                for kind in range(2):
                    link(dve.tensor_copy(maps[:, kind, 0, b, 1:1 + DC], largest[:, kind, :]))
                assert n_links == PER_BATCH
            step = 1

            def link(ins):
                nonlocal step
                step += 1
                ins.then_inc(tail, 1)
                dve.wait_ge(tail, step)

            dve.wait_ge(sums_done, B)
            dve.wait_ge(batch_split, B)
            for kind, n in ((0, TOP), (1, C - TOP)):
                v = maps[:, kind, 1, :, :]
                dve.tensor_scalar(v, v, 1.0 / C, float(C / n), ALU.mult, ALU.mult).then_inc(maps_scaled, 1)
            z = bank[0][:, 0:2 * B * DC].rearrange("p (k n) -> p k n", k=2)
            N = float(B * D)
            dve.wait_ge(z_done, 1)
            dve.tensor_reduce(zs[:, :], z, AX_X, ALU.add).then_inc(z_sums, 1)
            dve.wait_ge(z_done, 2)
            link(dve.tensor_scalar(zm[:, :], bank[1][:, 0:2], 1.0 / N, None, ALU.mult))
            for k in range(2):
                link(dve.tensor_scalar(zc[:, k, :], z[:, k, :], zm[:, k:k + 1], None, ALU.subtract))
            link(dve.tensor_tensor(zq[:, :, :], zc[:, :, :], zc[:, :, :], ALU.mult))
            dve.tensor_reduce(zs[:, :], zq[:, :, :], AX_X, ALU.add).then_inc(z_sums, 1)
            dve.wait_ge(z_done, 3)
            dve.tensor_scalar(zv[:, :], bank[1][:, 2:4], 1.0 / N, EPS_BN, ALU.mult, ALU.add).then_inc(z_var, 1)
            dve.wait_ge(z_rstd, 1)
            link(dve.tensor_scalar(zg[:, :], zr[:, :], bn[:, 0:1], None, ALU.mult))
            for k in range(2):
                link(dve.tensor_scalar(zc[:, k, :], zc[:, k, :], zg[:, k:k + 1], bn[:, 1:2], ALU.mult, ALU.add))
            dve.tensor_scalar(zc[:, :, :], zc[:, :, :], 0.0, None, ALU.max).then_inc(z_act_in, 1)
            dve.wait_ge(z_act, 1)
            link(dve.tensor_tensor(dcoef[:, :], coef[:, 0, :], coef[:, 1, :], ALU.subtract))


def phase_apply(nc, sb, ps, sem, sems, env):
    x, mask, mean_x, rstd_x, coef, dcoef, ident, resid = (
        env[k] for k in ("x", "mask", "mean_x", "rstd_x", "coef", "dcoef", "ident", "resid"))
    scope = ExitStack()
    with scope:
        x_in = [sb(f"ax_in{s}", [P, D], F32, scope) for s in range(CH)]
        gate = [sb(f"gate{q}", [P, DC, C], F32, scope) for q in range(2)]
        prod = [sb(f"prod{s}", [P, D], F32, scope) for s in range(CH)]
        bank = [ps(f"abank{i}", [P, 2 * HALF], scope) for i in range(4)]
        x_loaded, gate_ready, added = (sems(n) for n in ("ax_loaded", "gate_ready", "added"))
        turned, multiplied = (sems(n, 4) for n in ("a_turned", "multiplied"))
        block = scope.enter_context(nc.Block())

        @block.sync
        def _(sp):
            for b in rounds(sp, B):
                for h in range(CH):
                    sp.wait_ge(added[h], b)
                    sp.dma_start(x_in[h][:, :], x[b, h * P:(h + 1) * P, :]).then_inc(x_loaded[h], 16)

        @block.scalar
        def _(act):
            for p in rounds(act, B // 2):
                for q in range(2):
                    for h in range(CH):
                        act.wait_ge(turned[2 * q + h], p)
                    for c in range(DC):
                        n = (2 * p + q) * DC + c
                        last = act.activation(gate[q][:, c, :], mask[:, 2 * p + q, c, :], ACT.Identity,
                                              bias=coef[:, 1, bass.ds(n, 1)], scale=dcoef[:, bass.ds(n, 1)])
                    last.then_inc(gate_ready[q], 1)

        @block.tensor
        def _(pe):
            for p in rounds(pe, B // 2):
                for q in range(2):
                    pe.wait_ge(gate_ready[q], p + 1)
                    for h in range(CH):
                        pe.wait_ge(multiplied[2 * q + h], p)
                        for c in range(DC):
                            last = pe.transpose(bank[2 * q + h][:, c * P:(c + 1) * P],
                                                gate[q][:, c, h * P:(h + 1) * P], ident[:, :])
                        last.then_inc(turned[2 * q + h], 1)

        @block.vector
        def _(dve):
            for p in rounds(dve, B // 2):
                for q in range(2):
                    b = 2 * p + q
                    for h in range(CH):
                        dve.wait_ge(turned[2 * q + h], p + 1)
                        dve.wait_ge(x_loaded[h], 16 * b + 16)
                        dve.scalar_tensor_tensor(prod[h][:, :], x_in[h][:, :], mean_x[:, bass.ds(CH * b + h, 1)],
                                                 bank[2 * q + h][:, :], ALU.subtract, ALU.mult
                                                 ).then_inc(multiplied[2 * q + h], 1)
                    for h in range(CH):
                        dve.wait_ge(multiplied[2 * q + h], p + 1)
                        dve.scalar_tensor_tensor(resid[:, CH * b + h, :], prod[h][:, :],
                                                 rstd_x[:, bass.ds(CH * b + h, 1)], x_in[h][:, :],
                                                 ALU.mult, ALU.add).then_inc(added[h], 1)


def wait_alone(eng, settled, *waits):
    waits = [(s, v if isinstance(v, int) else eng.to_reg(v)) for s, v in waits]
    eng.wait_ge(settled, 1)
    for s, v in waits:
        eng.wait_ge(s, v)


class Norm:

    def __init__(self, nc, sb, ps, sems, resid, ident, minus_half, settled):
        self.settled = settled
        self.resid, self.ident, self.minus_half = resid, ident, minus_half
        self.stats = [sb(f"n_st{s}", [P, 2, 6]) for s in range(2)]
        self.mv = [sb(f"n_mv{s}", [P, 2]) for s in range(2)]
        self.ve = [sb(f"n_ve{s}", [P, 1]) for s in range(2)]
        self.rstd = [sb(f"n_rs{s}", [P, 1]) for s in range(2)]
        self.xn = [sb(f"n_xn{s}", [P, D]) for s in range(2)]
        self.hi = [sb(f"n_hi{s}", [P, D], F16) for s in range(2)]
        self.lo = [sb(f"n_lo{s}", [P, D], F16) for s in range(2)]
        self.part_stats = sems("n_part")
        self.stats_ready = sems("n_stats")
        self.eps_added = sems("n_eps")
        self.rstd_ready = sems("n_rstd")
        self.normed = sems("n_normed")
        self.turned = sems("n_turned")
        self.hi_ready = sems("n_hi")
        self.lo_ready = sems("n_lo")
        self.base = -NT // 2

    def phase(self, ps, scope, name, used):
        self.base += NT // 2
        self.turned_ps = ps(f"{name}_tps", [P, D], scope)
        self.used = used

    def so_far(self, p):
        return self.base + p

    def vector_norm(self, dve, tile):
        p, s = tile
        for k in range(2):
            last = dve.bn_stats(self.stats[s][:, k, :], self.resid[:, 2 * p + s, k * HALF:(k + 1) * HALF])
        last.then_inc(self.part_stats[s], 1)
        wait_alone(dve, self.settled, (self.part_stats[s], self.so_far(p + 1)))
        dve.bn_aggr(self.mv[s][:, :], self.stats[s][:, :, :]).then_inc(self.stats_ready[s], 1)
        dve.wait_ge(self.stats_ready[s], self.so_far(p + 1))
        dve.wait_ge(self.rstd_ready[s], self.so_far(p + 1))
        dve.wait_ge(self.turned[s], self.so_far(p))
        dve.tensor_scalar(self.xn[s][:, :], self.resid[:, 2 * p + s, :], self.mv[s][:, 0:1], self.rstd[s][:, :],
                          ALU.subtract, ALU.mult).then_inc(self.normed[s], 1)

    def pool_rstd(self, pool, tile):
        p, s = tile
        wait_alone(pool, self.settled, (self.stats_ready[s], self.so_far(p + 1)), (self.normed[s], self.so_far(p)))
        pool.tensor_scalar(self.ve[s][:, :], self.mv[s][:, 1:2], EPS_LN, None, ALU.add).then_inc(self.eps_added[s], 1)
        pool.wait_ge(self.eps_added[s], self.so_far(p + 1))
        pool.tensor_tensor(self.rstd[s][:, :], self.ve[s][:, :], self.minus_half[:, 0:1],
                           ALU.pow).then_inc(self.rstd_ready[s], 1)

    def tensor_turn(self, pe, tile):
        p, s = tile
        pe.wait_ge(self.normed[s], self.so_far(p + 1))
        if s == 0:
            pe.wait_ge(self.lo_ready[1], self.so_far(p))
        else:
            pe.wait_ge(self.lo_ready[0], self.so_far(p + 1))
        for c in range(DC):
            last = pe.transpose(self.turned_ps[:, c * P:(c + 1) * P], self.xn[s][:, c * P:(c + 1) * P],
                                self.ident[:, :])
        last.then_inc(self.turned[s], 1)

    def scalar_hi(self, act, tile):
        p, s = tile
        act.wait_ge(self.turned[s], self.so_far(p + 1))
        act.wait_ge(self.used[s], p)
        act.activation(self.hi[s][:, :], self.turned_ps[:, :], ACT.Copy).then_inc(self.hi_ready[s], 1)

    def vector_lo(self, dve, tile):
        p, s = tile
        dve.wait_ge(self.hi_ready[s], self.so_far(p + 1))
        dve.tensor_tensor(self.lo[s][:, :], self.turned_ps[:, :], self.hi[s][:, :],
                          ALU.subtract).then_inc(self.lo_ready[s], 1)


def product(pe, acc, pairs):
    for n, (w, m) in enumerate(pairs):
        last = pe.matmul(acc, w, m, start=(n == 0), stop=(n == len(pairs) - 1))
    return last


def down_pairs(norm, s, hi, lo):
    pairs = []
    for c in range(DC):
        x_hi, x_lo = norm.hi[s][:, c * P:(c + 1) * P], norm.lo[s][:, c * P:(c + 1) * P]
        pairs += [(x_hi, hi[:, c, :]), (x_hi, lo[:, c, :]), (x_lo, hi[:, c, :])]
    return pairs


def phase_lora(nc, sb, ps, sem, sems, env):
    resid, ident = env["resid"], env["ident"]
    down_hi, down_lo, up_hi, up_lo = (env[k][0] for k in ("down_hi", "down_lo", "up_hi", "up_lo"))
    scope = ExitStack()
    with scope:
        norm = env["norm"]
        logit, e, sc = ([sb(f"f_{n}{s}", [P, H], F32, scope) for s in range(2)] for n in ("logit", "e", "sc"))
        nmax, tot, inv = ([sb(f"f_{n}{s}", [P, 1], F32, scope) for s in range(2)] for n in ("nmax", "tot", "inv"))
        low = [sb(f"f_low{s}", [P, HR], F32, scope) for s in range(2)]
        low_hi = [sb(f"f_low_hi{s}", [P, HR], F16, scope) for s in range(2)]
        low_lo = [sb(f"f_low_lo{s}", [P, HR], F16, scope) for s in range(2)]
        small = [ps(f"f_small{s}", [P, HALF], scope) for s in range(2)]
        up_ps = [ps(f"f_up{s}", [P, D], scope) for s in range(2)]
        (low_ready, logit_ready, max_ready, exp_ready, inv_ready, score_ready, scaled, low_turned, low_hi_ready,
         low_lo_ready, up_ready, added) = (sems(f"f_{n}") for n in (
             "lowr", "logit", "max", "exp", "inv", "score", "scaled", "lturned", "lhi", "llo", "up", "added"))
        norm.phase(ps, scope, "f", low_ready)
        block = scope.enter_context(nc.Block())
        NP = NT // 2

        @block.gpsimd
        def _(pool):
            for p in rounds(pool, NP):
                for s in range(2):
                    norm.pool_rstd(pool, (p, s))

        @block.tensor
        def _(pe):
            def project(tile):
                p, s = tile
                pe.wait_ge(norm.lo_ready[s], norm.so_far(p + 1))
                pe.wait_ge(low_hi_ready[s], p)
                pe.wait_ge(low_lo_ready[s], p)
                last = product(pe, small[s][:, 0:WA], down_pairs(norm, s, down_hi, down_lo))
                last.then_inc(low_ready[s], 1)

            def rise(tile):
                p, s = tile
                pe.wait_ge(scaled[s], p + 1)
                pe.transpose(small[s][:, 256:256 + P], low[s][:, :], ident[:, :]).then_inc(low_turned[s], 1)
                pe.wait_ge(low_lo_ready[s], p + 1)
                pe.wait_ge(added[s], p)
                for n in range(2):
                    cols = slice(n * HALF, (n + 1) * HALF)
                    last = product(pe, up_ps[s][:, cols], [(low_hi[s][:, :], up_hi[:, cols]),
                                                           (low_hi[s][:, :], up_lo[:, cols]),
                                                           (low_lo[s][:, :], up_hi[:, cols])])
                last.then_inc(up_ready[s], 1)

            norm.tensor_turn(pe, (0, 0))
            for p in rounds(pe, NP - 1):
                for s in range(2):
                    norm.tensor_turn(pe, after((p, s)))
                    project((p, s))
                    rise((p, s))
            last = NP - 1
            norm.tensor_turn(pe, (last, 1))
            for s in range(2):
                project((last, s))
                rise((last, s))

        @block.scalar
        def _(act):
            def soft(tile):
                p, s = tile
                act.wait_ge(max_ready[s], p + 1)
                act.activation(e[s][:, :], logit[s][:, :], ACT.Exp, bias=nmax[s][:, :],
                               accum_out=tot[s][:, :]).then_inc(exp_ready[s], 1)
                act.wait_ge(low_turned[s], p + 1)
                act.wait_ge(up_ready[s], p)
                act.activation(low_hi[s][:, :], small[s][:, 256:256 + P], ACT.Copy).then_inc(low_hi_ready[s], 1)

            norm.scalar_hi(act, (0, 0))
            for p in rounds(act, NP - 1):
                for s in range(2):
                    norm.scalar_hi(act, after((p, s)))
                    soft((p, s))
            norm.scalar_hi(act, (NP - 1, 1))
            for s in range(2):
                soft((NP - 1, s))

        @block.vector
        def _(dve):
            def gate(tile):
                p, s = tile
                dve.wait_ge(low_ready[s], p + 1)
                dve.scalar_tensor_tensor(logit[s][:, :], small[s][:, HR:WA], 1.0 / WS, env["br_bc"][:, :],
                                         ALU.mult, ALU.add).then_inc(logit_ready[s], 1)
                dve.wait_ge(logit_ready[s], p + 1)
                dve.tensor_reduce(nmax[s][:, :], logit[s][:, :], AX_X, ALU.max, negate=True).then_inc(max_ready[s], 1)
                dve.wait_ge(exp_ready[s], p + 1)
                dve.reciprocal(inv[s][:, :], tot[s][:, :]).then_inc(inv_ready[s], 1)
                dve.wait_ge(inv_ready[s], p + 1)
                dve.tensor_scalar(sc[s][:, :], e[s][:, :], inv[s][:, :], LORA * H / WS, ALU.mult,
                                  ALU.mult).then_inc(score_ready[s], 1)
                dve.wait_ge(score_ready[s], p + 1)
                dve.tensor_tensor(low[s][:, :].rearrange("p (h r) -> p h r", h=H),
                                  small[s][:, 0:HR].rearrange("p (h r) -> p h r", h=H),
                                  sc[s][:, :].unsqueeze(2).broadcast_to([P, H, R]), ALU.mult).then_inc(scaled[s], 1)
                dve.wait_ge(low_hi_ready[s], p + 1)
                dve.tensor_tensor(low_lo[s][:, :], small[s][:, 256:256 + P], low_hi[s][:, :],
                                  ALU.subtract).then_inc(low_lo_ready[s], 1)

            def add(tile):
                p, s = tile
                dve.wait_ge(up_ready[s], p + 1)
                r = resid[:, 2 * p + s, :]
                dve.scalar_tensor_tensor(r, up_ps[s][:, :], 1.0 / WS, r, ALU.mult, ALU.add).then_inc(added[s], 1)

            norm.vector_norm(dve, (0, 0))
            norm.vector_norm(dve, (0, 1))
            norm.vector_lo(dve, (0, 0))
            for p in rounds(dve, NP - 1):
                for s in range(2):
                    norm.vector_norm(dve, (p + 1, s))
                    norm.vector_lo(dve, after((p, s)))
                    gate((p, s))
                    add((p, s))
            norm.vector_lo(dve, (NP - 1, 1))
            for s in range(2):
                gate((NP - 1, s))
                add((NP - 1, s))


def phase_attention(nc, sb, ps, sem, sems, env):
    resid, ident, ctx_in = env["resid"], env["ident"], env["ctx_in"]
    scope = ExitStack()
    with scope:
        norm = env["norm"]
        c_in = [sb(f"q_c_in{h}", [P, D], F32, scope) for h in range(CH)]
        part = env["shared"][:, :].rearrange("p (k j n) -> p k j n", k=4, j=2)
        v_hi, v_lo = ([part[:, k, j, :].rearrange("p (h d) -> p h d", h=CH) for j in range(2)] for k in (0, 1))
        k_hi, k_lo = ([part[:, k, j, :].rearrange("p (c n) -> p c n", c=DC) for j in range(2)] for k in (2, 3))
        nmax, tot, inv = ([sb(f"q_{n}{s}", [P, 1], F32, scope) for s in range(2)] for n in ("nmax", "tot", "inv"))
        e = [sb(f"q_e{s}", [P, C], F32, scope) for s in range(2)]
        e_hi = [sb(f"e_hi{s}", [P, C], F16, scope) for s in range(2)]
        e_lo = [sb(f"e_lo{s}", [P, C], F16, scope) for s in range(2)]
        k_ps = ps("k_ps", [P, D], scope)
        small = [ps(f"q_small{s}", [P, HALF], scope) for s in range(2)]
        o_ps = ps("o_ps", [P, D], scope)
        c_loaded, k_turned, k_hi_ready, k_lo_ready, v_hi_ready, v_lo_ready = (
            sems(f"q_{n}") for n in ("cin", "kturned", "khi", "klo", "vhi", "vlo"))
        (scored, max_ready, exp_ready, inv_ready, e_turned, e_hi_ready, e_lo_ready, mixed, added) = (
            sems(f"q_{n}") for n in ("scored", "max", "exp", "inv", "eturned", "ehi", "elo", "mixed", "added"))
        norm.phase(ps, scope, "q", scored)
        block = scope.enter_context(nc.Block())

        @block.sync
        def _(sp):
            for b in rounds(sp, B):
                for h in range(CH):
                    sp.wait_ge(k_turned[h], b)
                    sp.wait_ge(v_lo_ready[h], b)
                    sp.dma_start(c_in[h][:, :], ctx_in[b, h * P:(h + 1) * P, :]).then_inc(c_loaded[h], 16)

        @block.gpsimd
        def _(pool):
            def values(b, j):
                for h in range(CH):
                    wait_alone(pool, norm.settled, (c_loaded[h], 16 * b + 16))
                    pool.tensor_copy(v_hi[j][:, h, :], c_in[h][:, :]).then_inc(v_hi_ready[h], 1)
                    pool.wait_ge(v_hi_ready[h], b + 1)
                    pool.tensor_tensor(v_lo[j][:, h, :], c_in[h][:, :], v_hi[j][:, h, :],
                                       ALU.subtract).then_inc(v_lo_ready[h], 1)

            for s in range(CH):
                norm.pool_rstd(pool, (0, s))
            values(0, 0)
            for g in rounds(pool, B // 2 - 1):
                for j in range(2):
                    for s in range(CH):
                        norm.pool_rstd(pool, (2 * g + j + 1, s))
                    for s in range(CH):
                        pool.wait_ge(mixed[s], 2 * g + j)
                    values(2 * g + j + 1, (j + 1) % 2)
            for s in range(CH):
                norm.pool_rstd(pool, (B - 1, s))
            for s in range(CH):
                pool.wait_ge(mixed[s], B - 2)
            values(B - 1, 1)

        @block.tensor
        def _(pe):
            def turn_keys(b):
                for h in range(CH):
                    pe.wait_ge(c_loaded[h], 16 * b + 16)
                    if h == 0:
                        pe.wait_ge(k_lo_ready[1], b)
                        pe.wait_ge(k_hi_ready[1], b)
                    else:
                        pe.wait_ge(k_lo_ready[0], b + 1)
                        pe.wait_ge(k_hi_ready[0], b + 1)
                    for c in range(DC):
                        last = pe.transpose(k_ps[:, c * P:(c + 1) * P], c_in[h][:, c * P:(c + 1) * P], ident[:, :])
                    last.then_inc(k_turned[h], 1)

            def score(b, s, j):
                pe.wait_ge(norm.lo_ready[s], norm.so_far(b + 1))
                pe.wait_ge(k_lo_ready[1], b + 1)
                pe.wait_ge(e_hi_ready[s], b)
                pe.wait_ge(e_lo_ready[s], b)
                pairs = []
                for c in range(DC):
                    x_hi, x_lo = norm.hi[s][:, c * P:(c + 1) * P], norm.lo[s][:, c * P:(c + 1) * P]
                    pairs += [(x_hi, k_hi[j][:, c, :]), (x_hi, k_lo[j][:, c, :]), (x_lo, k_hi[j][:, c, :])]
                product(pe, small[s][:, 0:C], pairs).then_inc(scored[s], 1)

            def mix(b, s, j):
                pe.wait_ge(exp_ready[s], b + 1)
                for k in range(CH):
                    last = pe.transpose(small[s][:, C + k * P:C + (k + 1) * P], e[s][:, k * P:(k + 1) * P], ident[:, :])
                last.then_inc(e_turned[s], 1)
                pe.wait_ge(e_lo_ready[s], b + 1)
                for k in range(CH):
                    pe.wait_ge(v_lo_ready[k], b + 1)
                if s == 0:
                    pe.wait_ge(added[1], b)
                else:
                    pe.wait_ge(added[0], b + 1)
                for n in range(2):
                    cols = slice(n * HALF, (n + 1) * HALF)
                    pairs = []
                    for k in range(CH):
                        e_h, e_l = e_hi[s][:, k * P:(k + 1) * P], e_lo[s][:, k * P:(k + 1) * P]
                        pairs += [(e_h, v_hi[j][:, k, cols]), (e_h, v_lo[j][:, k, cols]), (e_l, v_hi[j][:, k, cols])]
                    last = product(pe, o_ps[:, cols], pairs)
                last.then_inc(mixed[s], 1)

            def batch(b, j, more):
                norm.tensor_turn(pe, (b, 1))
                score(b, 0, j)
                if more:
                    norm.tensor_turn(pe, (b + 1, 0))
                score(b, 1, j)
                mix(b, 0, j)
                if more:
                    turn_keys(b + 1)
                mix(b, 1, j)

            turn_keys(0)
            norm.tensor_turn(pe, (0, 0))
            for g in rounds(pe, B // 2 - 1):
                for j in range(2):
                    batch(2 * g + j, j, True)
            batch(B - 2, 0, True)
            batch(B - 1, 1, False)

        @block.scalar
        def _(act):
            def keys(b, j, first=False):
                if not first:
                    for s in range(CH):
                        act.wait_ge(scored[s], b - 1)
                for h in range(CH):
                    act.wait_ge(k_turned[h], b + 1)
                    act.activation(k_hi[j][:, :, h * P:(h + 1) * P], k_ps[:, :].rearrange("p (c n) -> p c n", c=DC),
                                   ACT.Copy).then_inc(k_hi_ready[h], 1)

            def soft(b, s):
                act.wait_ge(max_ready[s], b + 1)
                act.activation(e[s][:, :], small[s][:, 0:C], ACT.Exp, bias=nmax[s][:, :],
                               accum_out=tot[s][:, :]).then_inc(exp_ready[s], 1)

            def parts(b, s):
                act.wait_ge(e_turned[s], b + 1)
                act.wait_ge(mixed[s], b)
                act.activation(e_hi[s][:, :], small[s][:, C:2 * C], ACT.Copy).then_inc(e_hi_ready[s], 1)

            def batch(b, j, more):
                norm.scalar_hi(act, (b, 1))
                soft(b, 0)
                if more:
                    norm.scalar_hi(act, (b + 1, 0))
                soft(b, 1)
                parts(b, 0)
                if more:
                    keys(b + 1, (j + 1) % 2)
                parts(b, 1)

            keys(0, 0, True)
            norm.scalar_hi(act, (0, 0))
            for g in rounds(act, B // 2 - 1):
                for j in range(2):
                    batch(2 * g + j, j, True)
            batch(B - 2, 0, True)
            batch(B - 1, 1, False)

        @block.vector
        def _(dve):
            def keys(b, j):
                for h in range(CH):
                    dve.wait_ge(k_hi_ready[h], b + 1)
                    dve.tensor_tensor(k_lo[j][:, :, h * P:(h + 1) * P], k_ps[:, :].rearrange("p (c n) -> p c n", c=DC),
                                      k_hi[j][:, :, h * P:(h + 1) * P], ALU.subtract).then_inc(k_lo_ready[h], 1)

            def largest(b, s):
                dve.wait_ge(scored[s], b + 1)
                dve.tensor_reduce(nmax[s][:, :], small[s][:, 0:C], AX_X, ALU.max, negate=True).then_inc(max_ready[s], 1)
                dve.wait_ge(exp_ready[s], b + 1)
                dve.reciprocal(inv[s][:, :], tot[s][:, :]).then_inc(inv_ready[s], 1)

            def parts(b, s):
                dve.wait_ge(e_hi_ready[s], b + 1)
                dve.tensor_tensor(e_lo[s][:, :], small[s][:, C:2 * C], e_hi[s][:, :],
                                  ALU.subtract).then_inc(e_lo_ready[s], 1)

            def add(b, s):
                dve.wait_ge(mixed[s], b + 1)
                dve.wait_ge(inv_ready[s], b + 1)
                r = resid[:, CH * b + s, :]
                dve.scalar_tensor_tensor(r, o_ps[:, :], inv[s][:, :], r, ALU.mult, ALU.add).then_inc(added[s], 1)

            def batch(b, j, more):
                norm.vector_lo(dve, (b, 1))
                if more:
                    norm.vector_norm(dve, (b + 1, 0))
                largest(b, 0)
                if more:
                    norm.vector_lo(dve, (b + 1, 0))
                    norm.vector_norm(dve, (b + 1, 1))
                largest(b, 1)
                parts(b, 0)
                if more:
                    keys(b + 1, (j + 1) % 2)
                add(b, 0)
                parts(b, 1)
                add(b, 1)

            norm.vector_norm(dve, (0, 0))
            norm.vector_norm(dve, (0, 1))
            keys(0, 0)
            norm.vector_lo(dve, (0, 0))
            for g in rounds(dve, B // 2 - 1):
                for j in range(2):
                    batch(2 * g + j, j, True)
            batch(B - 2, 0, True)
            batch(B - 1, 1, False)


def phase_ffn(nc, sb, ps, sem, sems, env):
    resid, ident = env["resid"], env["ident"]
    base_hi, base_lo = env["base_hi"], env["base_lo"]
    down_hi, down_lo, up_hi, up_lo = (env[k][1] for k in ("down_hi", "down_lo", "up_hi", "up_lo"))
    out = env["out"].rearrange("b (h p) d -> (b h) p d", p=P)
    scope = ExitStack()
    with scope:
        norm = env["norm"]
        e, m8, rest, kept, comb = ([sb(f"g_{n}{s}", [P, H], F32, scope) for s in range(2)]
                                   for n in ("e", "m8", "rest", "kept", "comb"))
        nmax, den, inv = ([sb(f"g_{n}{s}", [P, 1], F32, scope) for s in range(2)] for n in ("nmax", "den", "inv"))
        low = [sb(f"g_low{s}", [P, HR], F32, scope) for s in range(2)]
        low_hi = [sb(f"g_low_hi{s}", [P, HR], F16, scope) for s in range(2)]
        low_lo = [sb(f"g_low_lo{s}", [P, HR], F16, scope) for s in range(2)]
        result = [sb(f"g_out{s}", [P, D], F32, scope) for s in range(2)]
        small = [ps(f"g_small{s}", [P, HALF], scope) for s in range(2)]
        o_ps = [ps(f"g_o{s}", [P, D], scope) for s in range(2)]
        (low_ready, max_ready, exp_ready, scaled, low_turned, low_hi_ready, low_lo_ready, mixed, biased,
         result_ready, stored, chain, comb_ready) = (sems(f"g_{n}") for n in (
             "lowr", "max", "exp", "scaled", "lturned", "lhi", "llo", "mixed", "biased", "result",
             "stored", "chain", "comb"))
        norm.phase(ps, scope, "g", mixed)
        LINKS = 8
        block = scope.enter_context(nc.Block())
        NP = NT // 2

        @block.gpsimd
        def _(pool):
            def bias(tile):
                p, s = tile
                wait_alone(pool, norm.settled, (norm.normed[s], norm.so_far(p + 1)))
                r = resid[:, 2 * p + s, :]
                pool.tensor_tensor(r, r, env["bias_bc"][:, :], ALU.add).then_inc(biased[s], 1)

            for s in range(2):
                norm.pool_rstd(pool, (0, s))
            for p in rounds(pool, NP - 1):
                for s in range(2):
                    norm.pool_rstd(pool, (p + 1, s))
                    bias((p, s))
            for s in range(2):
                bias((NP - 1, s))

        @block.tensor
        def _(pe):
            def project(tile):
                p, s = tile
                pe.wait_ge(norm.lo_ready[s], norm.so_far(p + 1))
                pe.wait_ge(low_hi_ready[s], p)
                pe.wait_ge(low_lo_ready[s], p)
                product(pe, small[s][:, 0:WA], down_pairs(norm, s, down_hi, down_lo)).then_inc(low_ready[s], 1)

            def based_on(tile, n):
                p, s = tile
                cols = slice(n * HALF, (n + 1) * HALF)
                for c in range(DC):
                    x_hi, x_lo = norm.hi[s][:, c * P:(c + 1) * P], norm.lo[s][:, c * P:(c + 1) * P]
                    for w, m in ((x_hi, base_hi), (x_hi, base_lo), (x_lo, base_hi)):
                        pe.matmul(o_ps[s][:, cols], w, m[:, c, cols], start=(c == 0 and w is x_hi and m is base_hi),
                                  stop=False)

            def rise(tile):
                p, s = tile
                pe.wait_ge(low_lo_ready[s], p + 1)
                for n in range(2):
                    cols = slice(n * HALF, (n + 1) * HALF)
                    pe.matmul(o_ps[s][:, cols], low_hi[s][:, :], up_hi[:, cols], start=False, stop=False)
                    pe.matmul(o_ps[s][:, cols], low_hi[s][:, :], up_lo[:, cols], start=False, stop=False)
                    last = pe.matmul(o_ps[s][:, cols], low_lo[s][:, :], up_hi[:, cols], start=False, stop=True)
                last.then_inc(mixed[s], 1)

            def tile_work(tile, more):
                p, s = tile
                project(tile)
                pe.wait_ge(result_ready[s], p)
                based_on(tile, 0)
                if more:
                    norm.tensor_turn(pe, after(tile))
                pe.wait_ge(scaled[s], p + 1)
                pe.transpose(small[s][:, 256:256 + P], low[s][:, :], ident[:, :]).then_inc(low_turned[s], 1)
                based_on(tile, 1)
                rise(tile)

            norm.tensor_turn(pe, (0, 0))
            for p in rounds(pe, NP - 1):
                for s in range(2):
                    tile_work((p, s), True)
            tile_work((NP - 1, 0), True)
            tile_work((NP - 1, 1), False)

        @block.scalar
        def _(act):
            def tile_work(tile, more):
                p, s = tile
                act.wait_ge(max_ready[s], p + 1)
                act.activation(e[s][:, :], small[s][:, HR:WA], ACT.Exp, bias=nmax[s][:, :],
                               scale=1.0 / WS).then_inc(exp_ready[s], 1)
                if more:
                    norm.scalar_hi(act, after(tile))
                act.wait_ge(low_turned[s], p + 1)
                act.wait_ge(mixed[s], p)
                act.activation(low_hi[s][:, :], small[s][:, 256:256 + P], ACT.Copy).then_inc(low_hi_ready[s], 1)

            norm.scalar_hi(act, (0, 0))
            for p in rounds(act, NP - 1):
                for s in range(2):
                    tile_work((p, s), True)
            tile_work((NP - 1, 0), True)
            tile_work((NP - 1, 1), False)

        @block.vector
        def _(dve):
            def gate(tile):
                p, s = tile
                dve.wait_ge(low_ready[s], p + 1)
                n = 0

                def link(ins):
                    nonlocal n
                    n += 1
                    ins.then_inc(chain[s], 1)
                    wait_alone(dve, norm.settled, (chain[s], LINKS * p + n))

                link(dve.tensor_reduce(nmax[s][:, :], small[s][:, HR:WA], AX_X, ALU.max, negate=True))
                dve.tensor_scalar(nmax[s][:, :], nmax[s][:, :], 1.0 / WS, None, ALU.mult).then_inc(max_ready[s], 1)
                wait_alone(dve, norm.settled, (exp_ready[s], p + 1))
                link(dve.max(m8[s][:, :], e[s][:, :]))
                link(dve.tensor_tensor(den[s][:, :], m8[s][:, 0:1], m8[s][:, 1:2], ALU.add))
                link(dve.memset(m8[s][:, 2:H], -5.0))
                link(dve.match_replace(rest[s][:, :], m8[s][:, :], e[s][:, :], -1.0))
                link(dve.reciprocal(inv[s][:, :], den[s][:, :]))
                link(dve.tensor_tensor(kept[s][:, :], rest[s][:, :], e[s][:, :], ALU.not_equal))
                link(dve.tensor_tensor(kept[s][:, :], kept[s][:, :], e[s][:, :], ALU.mult))
                assert n == LINKS
                dve.tensor_scalar(comb[s][:, :], kept[s][:, :], inv[s][:, :], LORA / WS, ALU.mult,
                                  ALU.mult).then_inc(comb_ready[s], 1)
                dve.wait_ge(comb_ready[s], p + 1)
                dve.tensor_tensor(low[s][:, :].rearrange("p (h r) -> p h r", h=H),
                                  small[s][:, 0:HR].rearrange("p (h r) -> p h r", h=H),
                                  comb[s][:, :].unsqueeze(2).broadcast_to([P, H, R]), ALU.mult).then_inc(scaled[s], 1)

            def parts(tile):
                p, s = tile
                dve.wait_ge(low_hi_ready[s], p + 1)
                dve.tensor_tensor(low_lo[s][:, :], small[s][:, 256:256 + P], low_hi[s][:, :],
                                  ALU.subtract).then_inc(low_lo_ready[s], 1)

            def finish(tile):
                p, s = tile
                dve.wait_ge(mixed[s], p + 1)
                dve.wait_ge(biased[s], p + 1)
                dve.wait_ge(stored[s], 16 * p)
                dve.scalar_tensor_tensor(result[s][:, :], o_ps[s][:, :], 1.0 / WS, resid[:, 2 * p + s, :],
                                         ALU.mult, ALU.add).then_inc(result_ready[s], 1)

            norm.vector_norm(dve, (0, 0))
            norm.vector_norm(dve, (0, 1))
            norm.vector_lo(dve, (0, 0))
            for p in rounds(dve, NP - 1):
                for s in range(2):
                    gate((p, s))
                    norm.vector_lo(dve, after((p, s)))
                    norm.vector_norm(dve, (p + 1, s))
                    parts((p, s))
                    finish((p, s))
            gate((NP - 1, 0))
            norm.vector_lo(dve, (NP - 1, 1))
            parts((NP - 1, 0))
            finish((NP - 1, 0))
            gate((NP - 1, 1))
            parts((NP - 1, 1))
            finish((NP - 1, 1))

        @block.sync
        def _(sp):
            for p in rounds(sp, NP):
                for s in range(2):
                    sp.wait_ge(result_ready[s], p + 1)
                    sp.dma_start(out[2 * p + s], result[s][:, :]).then_inc(stored[s], 16)
            for s in range(2):
                sp.wait_ge(stored[s], 16 * NP)


_INS = ["x", "ctx_4096", "L0_xattn_conv_w", "L0_xattn_bn_gamma", "L0_xattn_bn_beta", "L0_ffn_A", "L0_ffn_B",
        "L0_ffn_Wr", "L0_ffn_br", "L1_ffn_W_base", "L1_ffn_b_base", "L1_ffn_W_router", "L1_ffn_A_stack",
        "L1_ffn_B_stack"]


def kernel(**inputs):
    import numpy as _np
    import concourse.bacc as _bacc
    from concourse import mybir as _mybir
    from concourse.bass_utils import run_bass_kernel_spmd as _run

    nc = _bacc.Bacc("TRN2", target_bir_lowering=False, num_devices=1)
    arrays, args = {}, []
    for name in _INS:
        a = _np.ascontiguousarray(inputs[name])
        arrays[f"in_{name}_dram"] = a
        args.append(nc.dram_tensor(f"in_{name}_dram", a.shape, _mybir.dt.from_np(a.dtype), kind="ExternalInput").ap())
    out = nc.dram_tensor("out_0_dram", (B, C, D), F32, kind="ExternalOutput").ap()
    build_kernel(nc, *args, out)
    r = _run(nc, [arrays], core_ids=[0])
    return r.results[0]["out_0_dram"]
```

```python
from contextlib import ExitStack

import concourse.bass as bass
from concourse import mybir

ALU = mybir.AluOpType
ACT = mybir.ActivationFunctionType
AX_X = mybir.AxisListType.X
F32 = mybir.dt.float32
F16 = mybir.dt.float16
BF16 = mybir.dt.bfloat16
U8 = mybir.dt.uint8

P = 128
B = 8
C = 256
D = 1024
CH = C // P
DC = D // P
NT = B * CH
HALF = 512
TOP = 154
TAPS = 7
H = 8
R = 16
HR = H * R
WA = HR + H
EPS_LN = 1e-5
EPS_BN = 1e-5
WS = 64.0
LORA = 2.0
KS = 1.0 / 256.0
WINDOW = 8
AIM = 149.6
QUANTILE, DENSITY = 0.213, 0.39
NEAR_ENOUGH = 13.0
FOLDS = 4
LINKS_A_ROUND = 58
TAKEN = -3.4028234663852886e38


def build_kernel(nc, x, ctx_in, conv_w, bn_gamma, bn_beta, A0, B0, Wr0, br0, W_base, b_base, Wr1, A1, B1, out):
    stack = ExitStack()
    with stack:
        def sb(name, shape, dt=F32, scope=stack):
            return scope.enter_context(nc.sbuf_tensor(name, shape, dt))

        def ps(name, shape, scope, dt=F32):
            return scope.enter_context(nc.psum_tensor(name, shape, dt))

        def sem(name):
            return stack.enter_context(nc.semaphore(name))

        def sems(name, n=2):
            return [sem(f"{name}{i}") for i in range(n)]

        base_hi = sb("base_hi", [P, DC, D], F16)
        base_lo = sb("base_lo", [P, DC, D], F16)
        down_hi = [sb(f"down_hi{i}", [P, DC, WA], F16) for i in range(2)]
        down_lo = [sb(f"down_lo{i}", [P, DC, WA], F16) for i in range(2)]
        up_hi = [sb(f"up_hi{i}", [P, D], F16) for i in range(2)]
        up_lo = [sb(f"up_lo{i}", [P, D], F16) for i in range(2)]
        ident = sb("ident", [P, P])
        ones = sb("ones", [P, P])
        minus_half = sb("minus_half", [P, 2])
        br_bc = sb("br_bc", [P, H])
        bias_bc = sb("bias_bc", [P, D])

        const_ready = sem("const_ready")
        small_in = sem("small_in")

        mask = sb("mask", [P, B, DC, C], U8)
        mean_x = sb("mean_x", [P, NT])
        rstd_x = sb("rstd_x", [P, NT])
        coef = sb("coef", [P, 2, B * DC])
        dcoef = sb("dcoef", [P, B * DC])
        phase_channels(nc, sb, ps, sem, sems, locals())
        resid = sb("resid", [P, NT, D])
        phase_stream(nc, sb, ps, sem, sems, locals())


def phase_channels(nc, sb, ps, sem, sems, env):
    x, ctx_in, W_base = env["x"], env["ctx_in"], env["W_base"]
    ident, ones, minus_half = env["ident"], env["ones"], env["minus_half"]
    mask, mean_x, rstd_x, coef, dcoef = (env[k] for k in ("mask", "mean_x", "rstd_x", "coef", "dcoef"))
    const_ready, small_in = env["const_ready"], env["small_in"]
    scope = ExitStack()
    with scope:
        x_in = [[sb(f"x_in{j}{h}", [P, D], F32, scope) for h in range(CH)] for j in range(2)]
        c_in = [[sb(f"c_in{j}{h}", [P, D], F32, scope) for h in range(CH)] for j in range(2)]
        c_sq = [sb(f"c_sq{h}", [P, D], BF16, scope) for h in range(CH)]
        xn = [sb(f"xn{h}", [P, D], F32, scope) for h in range(CH)]
        ones16 = sb("ones16", [P, 1], BF16, scope)
        xt = [sb(f"xt{j}", [P, DC, C], F32, scope) for j in range(2)]
        keys = [sb(f"keys{j}", [P, DC, C], F32, scope) for j in range(2)]
        shut = [sb(f"shut{u}", [P, C], F32, scope) for u in range(DC)]
        cruc = sb("cruc", [P, DC, C], F32, scope)
        w_in = [cruc[:, 4 * s:4 * s + 4, :].rearrange("p u c -> p (u c)") for s in range(2)]
        compared = [sb(f"compared{j}", [P, DC, C], BF16, scope) for j in range(2)]
        taken = sb("taken", [P, DC, C], U8, scope)
        largest = sb("largest", [P, 2, DC], F32, scope)
        part_sums = sb("part_sums", [P, (B - 1) * DC, C >> FOLDS], F32, scope)
        top8 = sb("top8", [P, 8], F32, scope)
        work = sb("work", [P, C], F32, scope)
        near = sb("near", [P, DC, 8], F32, scope)
        pick = sb("pick", [P, DC, 8], F32, scope)
        order = sb("order", [P, 1, 8], F32, scope)
        rank = sb("rank", [P, DC], F32, scope)
        level = sb("level", [P, DC], F32, scope)
        last_key = sb("last_key", [P, DC], F32, scope)
        reached = sb("reached", [P, DC], F32, scope)
        wrong = sb("wrong", [P, DC], F32, scope)
        n_wrong = sb("n_wrong", [P, 1], F32, scope)
        failed = sb("failed", [1, 1], mybir.dt.int32, scope)
        small = {n: [sb(f"{n}{j}", [P, DC], F32, scope) for j in range(2)]
                 for n in ("lower", "signs", "gain", "off", "back", "bend", "far", "go", "m1", "v1", "sd")}
        lower, signs, gain, off, back, bend, far, go, m1, v1, sd = (
            small[n] for n in ("lower", "signs", "gain", "off", "back", "bend", "far", "go", "m1", "v1", "sd"))
        half_power = sb("half_power", [P, DC], F32, scope)
        stats = sb("stats", [P, CH, 2, 6], F32, scope)
        mv = sb("mv", [P, CH, 2], F32, scope)
        minus_mean = sb("minus_mean", [P, CH], F32, scope)
        shift = sb("shift", [P, CH], F32, scope)
        ve = sb("ve", [P, CH], F32, scope)
        rs = sb("rs", [P, CH], F32, scope)
        maps = sb("maps", [P, 2, 2, B, DC + 2], F32, scope)
        wide = sb("wide", [P, 384 + TAPS - 1], F32, scope)
        band = [sb(f"band{c}", [P, 384], F32, scope) for c in range(2)]
        taps = sb("taps", [P, 2 * TAPS], F32, scope)
        bn = sb("bn", [P, 2], F32, scope)
        zc = sb("zc", [P, 2, B * DC], F32, scope)
        zq = sb("zq", [P, 2, B * DC], F32, scope)
        zs = sb("zs", [P, 2], F32, scope)
        zm = sb("zm", [P, 2], F32, scope)
        zv = sb("zv", [P, 2], F32, scope)
        zr = sb("zr", [P, 2], F32, scope)
        zg = sb("zg", [P, 2], F32, scope)
        warm = sb("warm", [P, 1], F32, scope)
        x_ps = ps("x_ps", [P, 2 * HALF], scope)
        c_ps = ps("c_ps", [P, 2 * HALF], scope)
        w_ps = ps("w_ps", [P, D], scope)
        few_ps, some_ps = (ps(n, [P, HALF], scope) for n in ("few_ps", "some_ps"))
        mom_ps = [few_ps[:, 2 * DC * j:2 * DC * (j + 1)].rearrange("p (k u) -> p k u", k=2) for j in range(2)]
        sum_ps = some_ps[:, 0:B * DC]
        any_ps = some_ps[:, B * DC:B * DC + 1]

        w_loaded, w_turned = sems("w_loaded"), sems("w_turned")
        w_split, w_hi = sem("w_split"), sem("w_hi")
        x_loaded, c_loaded = ([sems(f"{n}{j}") for j in range(2)] for n in ("x_loaded", "c_loaded"))
        x_normed, squared = sem("x_normed"), sem("squared")
        x_stats, x_eps, x_rstd, x_shift, x_parts = (sem(n) for n in ("x_stats", "x_eps", "x_rstd", "x_shift", "x_parts"))
        x_turned, c_turned, xt_copied, keys_copied = (
            sem(n) for n in ("x_turned", "c_turned", "xt_copied", "keys_copied"))
        crucial_done = sem("crucial_done")
        moments, x_summed = sem("moments"), sem("x_summed")
        spread, rooted = sem("spread"), sem("rooted")
        aimed, counted = sems("aimed"), sems("counted")
        chain = sem("chain")
        proof, proved, proven, split, mapped = (
            sem(n) for n in ("proof", "proved", "proven", "split", "mapped"))
        mask_stored = sem("mask_stored")
        folded, taps_in, last_summed = sem("folded"), sem("taps_in"), sem("last_summed")
        tail, maps_scaled, z_done, z_sums, z_var, z_rstd, z_act_in, z_act = (
            sem(n) for n in ("tail", "maps_scaled", "z_done", "z_sums", "z_var", "z_rstd", "z_act_in", "z_act"))

        down_hi, down_lo, up_hi, up_lo = (env[k] for k in ("down_hi", "down_lo", "up_hi", "up_lo"))
        def into_down(i, c0, c1):
            d = {"hi": down_hi[i], "lo": down_lo[i]}
            return lambda part, half: d[part][:, 4 * half:4 * half + 4, c0:c1]

        def into_up(i):
            d = {"hi": up_hi[i], "lo": up_lo[i]}
            return lambda part, half: d[part][:, half * HALF:(half + 1) * HALF].rearrange("p (c n) -> p c n", c=4)

        items = []
        for i, (a, w, bm) in enumerate(((env["A0"], env["Wr0"], env["B0"]), (env["A1"], env["Wr1"], env["B1"]))):
            items.append((a.rearrange("h r d -> (h r) d"), HR, P, into_down(i, 0, HR), None))
            items.append((w, H, H, into_down(i, HR, WA), None))
            items.append((bm.rearrange("h (c p) r -> p c h r", p=P), P, P, into_up(i), "up"))
        arrived, per_slot = [], [0, 0]
        for n, item in enumerate(items):
            per_slot[n % 2] += 16 * (DC if item[4] == "up" else 1)
            arrived.append(per_slot[n % 2])

        def steps(eng, step, links=None):
            for b in (0, 1):
                step(0, b, b, True, True)
            if links is not None:
                entry = links["base"] + links["n"]
            with eng.Fori(1, B // 2 - 1) as g:
                if links is not None:
                    links["base"], links["n"] = entry + (g - 1) * LINKS_A_ROUND, 0
                for j in range(2):
                    step(g, j, 2, True, True)
            if links is not None:
                assert links["n"] == LINKS_A_ROUND, links["n"]
                links["base"], links["n"] = entry + (B // 2 - 2) * LINKS_A_ROUND, 0
            step(B // 2 - 1, 0, 2, True, True)
            step(B // 2 - 1, 1, 2, True, False)
            step(B // 2, 0, 2, False, False)
            step(B // 2, 1, 2, False, False)

        def before(g, j):
            return (g, 0) if j == 1 else (g - 1, 1)

        def next_to(g, j):
            return (g, 1) if j == 0 else (g + 1, 0)

        block = scope.enter_context(nc.Block())

        @block.sync
        def _(sp):
            sp.dma_start(taps[:, :], env["conv_w"].rearrange("a c t -> (a c t)").partition_broadcast(P)).then_inc(taps_in, 16)
            sp.dma_start(env["br_bc"][:, :], env["br0"].partition_broadcast(P)).then_inc(small_in, 16)
            sp.dma_start(env["bias_bc"][:, :], env["b_base"].partition_broadcast(P)).then_inc(small_in, 16)
            sp.dma_start(bn[:, 0:1], env["bn_gamma"].partition_broadcast(P)).then_inc(small_in, 16)
            sp.dma_start(bn[:, 1:2], env["bn_beta"].partition_broadcast(P)).then_inc(small_in, 16)

            def load_weights(n):
                src, rows, _, _, kind = items[n]
                s = n % 2
                sp.wait_ge(w_turned[s], n // 2)
                if kind == "up":
                    for c in range(DC):
                        sp.dma_start(w_in[s][:, c * P:(c + 1) * P].rearrange("p (h r) -> p h r", h=H),
                                     src[:, c]).then_inc(w_loaded[s], 16)
                else:
                    sp.dma_start(w_in[s][0:rows, :], src).then_inc(w_loaded[s], 16)

            def load(b, j, first=False):
                for h in range(CH):
                    if not first:
                        sp.wait_ge(c_turned, 4 * b - 4)
                    sp.dma_start(c_in[j][h][:, :], ctx_in[b, h * P:(h + 1) * P, :]).then_inc(c_loaded[j][h], 16)
                for h in range(CH):
                    if not first:
                        sp.wait_ge(x_normed, CH * b - CH)
                    sp.dma_start(x_in[j][h][:, :], x[b, h * P:(h + 1) * P, :]).then_inc(x_loaded[j][h], 16)

            for n in range(2):
                load_weights(n)
            load(1, 1, True)
            load_weights(2)
            load(2, 0)
            for n in range(3, len(items)):
                load_weights(n)
            load(3, 1)
            with sp.Fori(2, B // 2) as g:
                for j in range(2):
                    load(2 * g + j, j)

        @block.scalar
        def _(act):
            for h in range(CH):
                act.dma_start(c_in[0][h][:, :], ctx_in[0, h * P:(h + 1) * P, :]).then_inc(c_loaded[0][h], 16)
                act.dma_start(x_in[0][h][:, :], x[0, h * P:(h + 1) * P, :]).then_inc(x_loaded[0][h], 16)

            def hi_parts(n):
                _, _, cols, dest, _ = items[n]
                s = n % 2
                act.wait_ge(w_turned[s], n // 2 + 1)
                for half in range(2):
                    src = w_ps[:, half * HALF:(half + 1) * HALF].rearrange("p (c n) -> p c n", c=4)[:, :, 0:cols]
                    last = act.activation(dest("hi", half), src, ACT.Copy, scale=WS)
                last.then_inc(w_hi, 1)

            def count(g, j, i, behind=2, here=False):
                act.wait_ge(aimed[j], 5 * g + i + 1)
                for u in range(DC):
                    last = act.activation(compared[j][:, u, :], keys[j][:, u, :], ACT.Sign, bias=lower[j][:, u:u + 1],
                                          accum_out=signs[j][:, u:u + 1])
                last.then_inc(counted[j], 1)
                if behind < 2 and here and 4 * j + i < len(items):
                    hi_parts(4 * j + i)

            def copy_keys(b, j):
                for n in range(4):
                    act.wait_ge(c_turned, 4 * b + n + 1)
                    act.activation(keys[j][:, 2 * n:2 * n + 2, :],
                                   c_ps[:, (n % 2) * HALF:(n % 2 + 1) * HALF].rearrange("p (u c) -> p u c", u=2),
                                   ACT.Copy, scale=KS).then_inc(keys_copied, 1)

            def copy_x(b, j, groups):
                for n in groups:
                    act.wait_ge(x_turned, 4 * b + n + 1)
                    act.activation(xt[j][:, 2 * n:2 * n + 2, :],
                                   x_ps[:, (n % 2) * HALF:(n % 2 + 1) * HALF].rearrange("p (u c) -> p u c", u=2),
                                   ACT.Copy).then_inc(xt_copied, 1)

            def step(g, j, behind, here, ahead):
                b = 2 * g + j
                old = behind >= 1 and (here or j == 0)
                if here:
                    act.wait_ge(keys_copied, 4 * b + 4)
                    count(g, j, 0, behind, here)
                if old:
                    count(*before(g, j), 4)
                if here:
                    count(g, j, 1, behind, here)
                    if behind >= 2:
                        act.wait_ge(split, b - 1)
                    copy_x(b, j, (0, 1, 2))
                    count(g, j, 2, behind, here)
                    copy_x(b, j, (3,))
                if here:
                    count(g, j, 3, behind, here)
                if old:
                    act.wait_ge(proven, b)
                    act.dma_start(mask[:, b - 1, :, :], taken[:, :, :]).then_inc(mask_stored, 16)
                if ahead:
                    copy_keys(b + 1, (j + 1) % 2)
                if not here and j == 1:
                    for u in range(DC):
                        act.wait_ge(crucial_done, DC * (B - 1) + u + 1)
                        last = act.activation(compared[0][:, u, :], cruc[:, u, :], ACT.Copy,
                                              accum_out=maps[:, 0, 1, B - 1, 1 + u:2 + u])
                    last.then_inc(last_summed, 1)

            copy_keys(0, 0)
            steps(act, step)
            act.activation(warm[:, :], ones[:, 0:1], ACT.Sigmoid)
            act.wait_ge(mask_stored, 16 * B)
            act.wait_ge(z_act_in, 1)
            act.activation(coef[:, :, :], zc[:, :, :], ACT.Sigmoid).then_inc(z_act, 1)

        @block.gpsimd
        def _(pool):
            pool.memset(ident[:, :], 0.0).then_inc(const_ready, 1)
            pool.memset(wide[:, :], 0.0).then_inc(const_ready, 1)
            pool.memset(ones[:, :], 1.0).then_inc(const_ready, 1)
            pool.memset(minus_half[:, :], -0.5).then_inc(const_ready, 1)
            pool.memset(half_power[:, :], 0.5).then_inc(const_ready, 1)
            pool.memset(ones16[:, :], 1.0).then_inc(const_ready, 1)
            for k in range(8):
                pool.memset(order[:, :, k:k + 1], k + 1.0).then_inc(const_ready, 1)
            pool.wait_ge(const_ready, 14)
            pool.affine_select(out=ident[:, :], in_=ident[:, :], compare_op=ALU.not_equal, fill=1.0, base=0,
                               pattern=[[-1, P]], channel_multiplier=1).then_inc(const_ready, 1)
            pool.affine_select(out=wide[:, :], in_=wide[:, :], compare_op=ALU.not_equal, fill=1.0,
                               base=131, pattern=[[-1, 384 + TAPS - 1]], channel_multiplier=1).then_inc(const_ready, 1)
            pool.wait_ge(const_ready, 16)

            def square(g, j):
                for h in range(CH):
                    wait_alone(pool, const_ready, (c_loaded[j][h], 16 * g + 16), (moments, 2 * g + j))
                    pool.tensor_tensor(c_sq[h][:, :], c_in[j][h][:, :], c_in[j][h][:, :], ALU.mult).then_inc(squared, 1)

            def root(b, j):
                wait_alone(pool, const_ready, (spread, b + 1))
                pool.tensor_tensor(sd[j][:, :], v1[j][:, :], half_power[:, :], ALU.pow).then_inc(rooted, 1)

            def scale_and_shift(b):
                wait_alone(pool, const_ready, (x_stats, b + 1))
                pool.tensor_scalar(ve[:, :], mv[:, :, 1], EPS_LN, None, ALU.add).then_inc(x_eps, 1)
                wait_alone(pool, const_ready, (x_eps, b + 1), (x_normed, CH * b))
                pool.tensor_tensor(rs[:, :], ve[:, :], minus_half[:, :], ALU.pow).then_inc(x_rstd, 1)
                pool.tensor_scalar(minus_mean[:, :], mv[:, :, 0], -1.0, None, ALU.mult).then_inc(x_rstd, 1)
                wait_alone(pool, const_ready, (x_rstd, 2 * b + 2))
                pool.tensor_tensor(shift[:, :], minus_mean[:, :], rs[:, :], ALU.mult).then_inc(x_shift, 1)
                pool.tensor_copy(rstd_x[:, bass.ts(b, CH)], rs[:, :]).then_inc(x_shift, 1)
                pool.tensor_copy(mean_x[:, bass.ts(b, CH)], mv[:, :, 0]).then_inc(x_shift, 1)

            def normalise(b, j):
                wait_alone(pool, const_ready, (x_shift, 3 * b + 3), (x_turned, 4 * b), (x_summed, b))
                for h in range(CH):
                    pool.tensor_scalar(xn[h][:, :], x_in[j][h][:, :], rs[:, h:h + 1], shift[:, h:h + 1], ALU.mult,
                                       ALU.add).then_inc(x_normed, 1)

            def gather(b):
                wait_alone(pool, const_ready, (split, b + 1))
                pool.tensor_copy(maps[:, 0, 0, b, 1:1 + DC], largest[:, 0, :]).then_inc(mapped, 1)
                pool.tensor_copy(maps[:, 1, 0, b, 1:1 + DC], largest[:, 1, :]).then_inc(mapped, 1)
                if isinstance(b, int) and b == B - 1:
                    return
                width = C // 2
                for n in range(FOLDS - 1):
                    pool.tensor_tensor(cruc[:, :, 0:width], cruc[:, :, 0:width], cruc[:, :, width:2 * width],
                                       ALU.add).then_inc(folded, 1)
                    width //= 2
                    wait_alone(pool, const_ready, (folded, (FOLDS - 1) * b + n + 1))
                pool.tensor_tensor(part_sums[:, bass.ts(b, DC), :], cruc[:, :, 0:width], cruc[:, :, width:2 * width],
                                   ALU.add).then_inc(mapped, 1)

            def step(g, j, behind, here, ahead):
                b = 2 * g + j
                if ahead:
                    square(*next_to(g, j))
                    scale_and_shift(b + 1)
                if behind >= 2:
                    gather(b - 2)
                if ahead:
                    normalise(b + 1, (j + 1) % 2)
                    root(b + 1, (j + 1) % 2)

            square(0, 0)
            scale_and_shift(0)
            normalise(0, 0)
            root(0, 0)
            pool.wait_ge(mapped, 1)
            steps(pool, step)
            pool.wait_ge(z_var, 1)
            pool.tensor_tensor(zr[:, :], zv[:, :], minus_half[:, :], ALU.pow).then_inc(z_rstd, 1)

        @block.tensor
        def _(pe):
            pe.wait_ge(const_ready, 16)

            def turn_weights(n):
                _, rows, cols, _, _ = items[n]
                s = n % 2
                pe.wait_ge(w_loaded[s], arrived[n])
                pe.wait_ge(w_split, n)
                for c in range(DC):
                    last = pe.transpose(w_ps[:, c * P:c * P + cols], w_in[s][0:rows, c * P:(c + 1) * P],
                                        ident[0:rows, 0:rows])
                last.then_inc(w_turned[s], 1)

            def turn(b, n, dst, src, turned, copied, first=False):
                if not (first and n < 2):
                    pe.wait_ge(copied, 4 * b + n - 1)
                for u in range(2):
                    for h in range(CH):
                        at, c = (n % 2) * HALF + u * C + h * P, 2 * n + u
                        last = pe.transpose(dst[:, at:at + P], src[h][:, c * P:(c + 1) * P], ident[:, :])
                last.then_inc(turned, 1)

            def turn_x(b, groups, first=False):
                pe.wait_ge(x_normed, CH * b + CH)
                for n in groups:
                    turn(b, n, x_ps, xn, x_turned, xt_copied, first)

            def turn_keys(g, j, groups, first=False):
                for h in range(CH):
                    pe.wait_ge(c_loaded[j][h], 16 * g + 16)
                for n in groups:
                    turn(2 * g + j, n, c_ps, c_in[j], c_turned, keys_copied, first)

            def sum_keys(b, j, first=False):
                pe.wait_ge(squared, CH * b + CH)
                if not first:
                    pe.wait_ge(spread, b - 1)
                for c in range(DC):
                    for h in range(CH):
                        pe.matmul(mom_ps[j][:, 0, c:c + 1], c_in[j][h][:, c * P:(c + 1) * P], ones[:, 0:1],
                                  start=(h == 0), stop=(h == CH - 1))
                    for h in range(CH):
                        last = pe.matmul(mom_ps[j][:, 1, c:c + 1], c_sq[h][:, c * P:(c + 1) * P], ones16[:, :],
                                         start=(h == 0), stop=(h == CH - 1))
                last.then_inc(moments, 1)

            def sum_x(b, chunks):
                for c in chunks:
                    for h in range(CH):
                        last = pe.matmul(sum_ps[:, bass.ds(DC * b + c, 1)], xn[h][:, c * P:(c + 1) * P], ones[:, 0:1],
                                         start=(h == 0), stop=(h == CH - 1))
                if DC - 1 in chunks:
                    last.then_inc(x_summed, 1)

            def step(g, j, behind, here, ahead):
                b = 2 * g + j
                weights = range(4 * b, min(4 * b + 4, len(items))) if behind < 2 else ()
                for n in weights[0:1]:
                    turn_weights(n)
                if here:
                    turn_x(b, (0, 1), behind == 0)
                for n in weights[1:2]:
                    turn_weights(n)
                if ahead:
                    sum_keys(b + 1, (j + 1) % 2, behind == 0)
                if here:
                    sum_x(b, range(DC // 2))
                    turn_x(b, (2, 3))
                    sum_x(b, range(DC // 2, DC))
                for n in weights[2:3]:
                    turn_weights(n)
                if ahead:
                    turn_keys(*next_to(g, j), (0, 1))
                for n in weights[3:4]:
                    turn_weights(n)
                if behind >= 1 and (here or j == 0):
                    pe.wait_ge(proof, b)
                    pe.matmul(any_ps[:, :], ones[:, :], n_wrong[:, :], start=True, stop=True).then_inc(proved, 1)
                if ahead:
                    turn_keys(*next_to(g, j), (2, 3))

            sum_keys(0, 0, True)
            turn_keys(0, 0, range(4), True)
            steps(pe, step)
            pe.wait_ge(mapped, 3 * B)
            pe.wait_ge(maps_scaled, 2)
            pe.wait_ge(chain, 2 * TAPS)
            n = 0
            for ch in range(2):
                for shift, at in ((0, 256), (1, 128), (2, 0)):
                    n += 1
                    last = pe.matmul(x_ps[:, 0:2 * B * DC].rearrange("p (k b c) -> p k b c", k=2, b=B),
                                     band[ch][:, at:at + P], maps[:, :, ch, :, shift:shift + DC],
                                     start=(n == 1), stop=(n == 6))
            last.then_inc(z_done, 1)
            for n in range(2):
                pe.wait_ge(z_sums, n + 1)
                pe.matmul(c_ps[:, 2 * n:2 * n + 2], ones[:, :], zs[:, :], start=True, stop=True).then_inc(z_done, 1)

        @block.vector
        def _(dve):
            dve.wait_ge(taps_in, 16)
            dve.wait_ge(const_ready, 16)
            LEAD = 2 * TAPS
            for ch in range(2):
                for t in range(TAPS):
                    w = taps[:, ch * TAPS + t:ch * TAPS + t + 1]
                    if t == 0:
                        ins = dve.tensor_scalar(band[ch][:, :], wide[:, 0:384], w, None, ALU.mult)
                    else:
                        ins = dve.scalar_tensor_tensor(band[ch][:, :], wide[:, t:t + 384], w, band[ch][:, :],
                                                       ALU.mult, ALU.add)
                    ins.then_inc(chain, 1)
                    dve.wait_ge(chain, ch * TAPS + t + 1)

            def lo_parts(n):
                _, _, cols, dest, _ = items[n]
                dve.wait_ge(w_hi, n + 1)
                for half in range(2):
                    src = w_ps[:, half * HALF:(half + 1) * HALF].rearrange("p (c n) -> p c n", c=4)[:, :, 0:cols]
                    last = dve.scalar_tensor_tensor(dest("lo", half), src, WS, dest("hi", half), ALU.mult, ALU.subtract)
                last.then_inc(w_split, 1)

            dve.wait_ge(small_in, 64)
            dve.memset(maps[:, :, :, :, :].rearrange("p a b c d -> p (a b c d)"), 0.0).then_inc(mapped, 1)
            links = {"base": LEAD, "n": 0}

            def link(ins, between=None):
                links["n"] += 1
                own = links["base"] + links["n"]
                ins.then_inc(chain, 1)
                if between is not None:
                    next(between, None)
                wait_alone(dve, const_ready, (chain, own))

            def first_aim(b, j):
                dve.wait_ge(moments, b + 1)
                link(dve.tensor_scalar(m1[j][:, :], mom_ps[j][:, 0, :], KS / C, None, ALU.mult))
                link(dve.tensor_tensor(bend[j][:, :], m1[j][:, :], m1[j][:, :], ALU.mult))
                link(dve.scalar_tensor_tensor(v1[j][:, :], mom_ps[j][:, 1, :], KS * KS / C, bend[j][:, :], ALU.mult,
                                              ALU.subtract))
                dve.tensor_scalar(v1[j][:, :], v1[j][:, :], 0.0, None, ALU.max).then_inc(spread, 1)

            def first_aim_end(b, j):
                dve.wait_ge(rooted, b + 1)
                dve.tensor_scalar(gain[j][:, :], sd[j][:, :], -1.0 / (C * DENSITY), None, ALU.mult)
                dve.scalar_tensor_tensor(lower[j][:, :], sd[j][:, :], QUANTILE, m1[j][:, :], ALU.mult,
                                         ALU.subtract).then_inc(aimed[j], 1)

            def steer_by(g, j, i, between=None):
                dve.wait_ge(counted[j], 5 * g + i + 1)
                link(dve.tensor_scalar(off[j][:, :], signs[j][:, :], 0.5, C / 2.0 - AIM, ALU.mult, ALU.add), between)
                far_off = dve.tensor_tensor(far[j][:, :], off[j][:, :], off[j][:, :], ALU.mult)
                if i == 0:
                    link(far_off, between)
                else:
                    link(dve.scalar_tensor_tensor(bend[j][:, :], off[j][:, :], -1.0, back[j][:, :], ALU.mult,
                                                  ALU.mult), between)
                away = dve.scalar_tensor_tensor(go[j][:, :], far[j][:, :], NEAR_ENOUGH, off[j][:, :], ALU.is_gt, ALU.mult)
                if i == 0:
                    link(away, between)
                else:
                    link(dve.tensor_scalar(bend[j][:, :], bend[j][:, :], 1.0, 0.5, ALU.add, ALU.max), between)
                dve.reciprocal(back[j][:, :], off[j][:, :])
                step_by = dve.tensor_tensor(go[j][:, :], go[j][:, :], gain[j][:, :], ALU.mult)
                if i == 0:
                    link(step_by, between)
                else:
                    link(dve.reciprocal(bend[j][:, :], bend[j][:, :]), between)
                    link(dve.tensor_tensor(go[j][:, :], go[j][:, :], bend[j][:, :], ALU.mult), between)
                dve.tensor_tensor(lower[j][:, :], lower[j][:, :], go[j][:, :], ALU.add).then_inc(aimed[j], 1)
                if i > 0:
                    dve.tensor_tensor(gain[j][:, :], gain[j][:, :], bend[j][:, :], ALU.mult)
                for _ in between or ():
                    pass

            def level_of(g, j):
                dve.wait_ge(counted[j], 5 * g + 5)
                dve.tensor_scalar(rank[:, :], signs[j][:, :], -0.5, TOP - C / 2.0, ALU.mult, ALU.add)
                link(dve.tensor_scalar(level[:, :], lower[j][:, :], -1.0, None, ALU.mult))


            def put_away(j):
                for u in range(DC):
                    last = dve.scalar_tensor_tensor(shut[u][:, :], keys[j][:, u, :], level[:, u:u + 1],
                                                    keys[j][:, u, :], ALU.is_ge, ALU.subtract, reverse1=True)
                link(last)

            def nearest():
                for u in range(DC):
                    dve.max(near[:, u, :], shut[u][:, :])
                    yield

            def crucial(j):
                for u in range(DC):
                    dve.tensor_tensor_reduce(out=cruc[:, u, :], in0=taken[:, u, :], in1=xt[j][:, u, :], scale=1.0,
                                             scalar=TAKEN, op0=ALU.mult, op1=ALU.max,
                                             accum_out=largest[:, 0, u:u + 1]).then_inc(crucial_done, 1)
                    yield

            def subcrucial(j, entered):
                for u in range(DC):
                    wait_alone(dve, const_ready, (crucial_done, entered + u + 1))
                    last = dve.tensor_tensor_reduce(out=shut[u][:, :], in0=xt[j][:, u, :], in1=cruc[:, u, :], scale=1.0,
                                                    scalar=TAKEN, op0=ALU.subtract, op1=ALU.max,
                                                    accum_out=largest[:, 1, u:u + 1])
                    yield
                last.then_inc(split, 1)

            def end_key(b):
                link(dve.tensor_tensor(pick[:, :, :], order[:, :, :].broadcast_to([P, DC, 8]),
                                       rank[:, :].unsqueeze(2).broadcast_to([P, DC, 8]), ALU.is_equal))
                link(dve.tensor_tensor(pick[:, :, :], pick[:, :, :], near[:, :, :], ALU.mult))
                link(dve.tensor_reduce(last_key[:, :], pick[:, :, :], AX_X, ALU.add))
                dve.wait_ge(mask_stored, 16 * b)

            def reach(j, units):
                for u in units:
                    last = dve.tensor_scalar(taken[:, u, :], keys[j][:, u, :], last_key[:, u:u + 1], None, ALU.is_ge,
                                             ALU.add, accum_out=reached[:, u:u + 1])
                    yield
                if DC - 1 in units:
                    link(last)

            def prove():
                dve.tensor_scalar(wrong[:, :], reached[:, :], float(TOP), None, ALU.not_equal, ALU.add,
                                  accum_out=n_wrong[:, :]).then_inc(proof, 1)

            def settle(b, j):
                dve.wait_ge(proved, b + 1)
                link(dve.tensor_copy(failed[:, :], any_ps[0:1, :]))
                again = dve.value_load(failed[0:1, 0:1], min_val=0, max_val=P * DC)
                n_rounds = (TOP + 7) // 8
                left = TOP - 8 * (n_rounds - 1)
                with dve.If(again > 0):
                    for u in range(DC):
                        dve.max(top8[:, :], keys[j][:, u, :])
                        dve.drain()
                        dve.match_replace(work[:, :], top8[:, :], keys[j][:, u, :], TAKEN)
                        dve.drain()
                        with dve.Fori(0, n_rounds - 2):
                            dve.max(top8[:, :], work[:, :])
                            dve.drain()
                            dve.match_replace(work[:, :], top8[:, :], work[:, :], TAKEN)
                            dve.drain()
                        dve.max(top8[:, :], work[:, :])
                        dve.drain()
                        dve.memset(top8[:, left:8], TAKEN)
                        dve.drain()
                        dve.match_replace(work[:, :], top8[:, :], work[:, :], TAKEN)
                        dve.drain()
                        dve.tensor_tensor(taken[:, u, :], work[:, :], keys[j][:, u, :], ALU.not_equal)
                        dve.drain()
                dve.sem_inc(proven, 1)

            def x_statistics(g, j):
                b = 2 * g + j
                for h in range(CH):
                    dve.wait_ge(x_loaded[j][h], 16 * g + 16)
                    for k in range(2):
                        last = dve.bn_stats(stats[:, h, k, :], x_in[j][h][:, k * HALF:(k + 1) * HALF])
                last.then_inc(x_parts, 1)
                wait_alone(dve, const_ready, (x_parts, b + 1), (x_shift, 3 * b))
                for h in range(CH):
                    last = dve.bn_aggr(mv[:, h, :], stats[:, h, :, :])
                last.then_inc(x_stats, 1)

            def step(g, j, behind, here, ahead):
                b = 2 * g + j
                prev = before(g, j)
                old = behind >= 1 and (here or j == 0)
                if behind >= 2:
                    wait_alone(dve, const_ready, (xt_copied, 4 * b - 4), (mapped, 3 * b - 5))
                if old:
                    steer_by(*prev, 3, crucial(j) if behind >= 2 else None)
                elif behind >= 2:
                    for _ in crucial(j):
                        pass
                weights = range(4 * b, min(4 * b + 3, len(items))) if behind < 2 else ()
                if behind == 1 and 4 * b - 1 < len(items):
                    lo_parts(4 * b - 1)
                if ahead:
                    x_statistics(*next_to(g, j))
                if here:
                    steer_by(g, j, 0, subcrucial(j, DC * (b - 2)) if behind >= 2 else None)
                    for n in weights[0:1]:
                        lo_parts(n)
                elif behind >= 2:
                    for _ in subcrucial(j, DC * (b - 2)):
                        pass
                if old:
                    level_of(*prev)
                    put_away(prev[1])
                if here:
                    steer_by(g, j, 1, nearest() if old else None)
                    for n in weights[1:2]:
                        lo_parts(n)
                elif old:
                    for _ in nearest():
                        pass
                if old:
                    end_key(b - 1)
                    for _ in reach(prev[1], range(DC // 2)):
                        pass
                if here:
                    steer_by(g, j, 2)
                    for n in weights[2:3]:
                        lo_parts(n)
                if old:
                    for _ in reach(prev[1], range(DC // 2, DC)):
                        pass
                if old:
                    prove()
                if ahead:
                    first_aim(b + 1, (j + 1) % 2)
                if old:
                    settle(b - 1, prev[1])
                if ahead:
                    first_aim_end(b + 1, (j + 1) % 2)

            x_statistics(0, 0)
            first_aim(0, 0)
            first_aim_end(0, 0)
            steps(dve, step, links)

            t = {"n": 0}

            def then(ins):
                t["n"] += 1
                ins.then_inc(tail, 1)
                dve.wait_ge(tail, t["n"])

            dve.wait_ge(mapped, 3 * (B - 1) + 1)
            then(dve.tensor_reduce(maps[:, 0, 1, 0:B - 1, 1:1 + DC],
                                   part_sums[:, :, :].rearrange("p (b c) n -> p b c n", b=B - 1), AX_X, ALU.add))
            dve.wait_ge(last_summed, 1)
            dve.wait_ge(mapped, 3 * B)
            dve.wait_ge(x_summed, B)
            then(dve.tensor_tensor(maps[:, 1, 1, :, 1:1 + DC], sum_ps[:, 0:B * DC].rearrange("p (b c) -> p b c", b=B),
                                   maps[:, 0, 1, :, 1:1 + DC], ALU.subtract))
            for kind, n in ((0, TOP), (1, C - TOP)):
                v = maps[:, kind, 1, :, :]
                dve.tensor_scalar(v, v, 1.0 / C, float(C / n), ALU.mult, ALU.mult).then_inc(maps_scaled, 1)
            z = x_ps[:, 0:2 * B * DC].rearrange("p (k n) -> p k n", k=2)
            N = float(B * D)
            dve.wait_ge(z_done, 1)
            dve.tensor_reduce(zs[:, :], z, AX_X, ALU.add).then_inc(z_sums, 1)
            dve.wait_ge(z_done, 2)
            then(dve.tensor_scalar(zm[:, :], c_ps[:, 0:2], 1.0 / N, None, ALU.mult))
            for k in range(2):
                then(dve.tensor_scalar(zc[:, k, :], z[:, k, :], zm[:, k:k + 1], None, ALU.subtract))
            then(dve.tensor_tensor(zq[:, :, :], zc[:, :, :], zc[:, :, :], ALU.mult))
            dve.tensor_reduce(zs[:, :], zq[:, :, :], AX_X, ALU.add).then_inc(z_sums, 1)
            dve.wait_ge(z_done, 3)
            dve.tensor_scalar(zv[:, :], c_ps[:, 2:4], 1.0 / N, EPS_BN, ALU.mult, ALU.add).then_inc(z_var, 1)
            dve.wait_ge(z_rstd, 1)
            then(dve.tensor_scalar(zg[:, :], zr[:, :], bn[:, 0:1], None, ALU.mult))
            for k in range(2):
                then(dve.tensor_scalar(zc[:, k, :], zc[:, k, :], zg[:, k:k + 1], bn[:, 1:2], ALU.mult, ALU.add))
            dve.tensor_scalar(zc[:, :, :], zc[:, :, :], 0.0, None, ALU.max).then_inc(z_act_in, 1)
            dve.wait_ge(z_act, 1)
            then(dve.tensor_tensor(dcoef[:, :], coef[:, 0, :], coef[:, 1, :], ALU.subtract))


def since(eng, *waits):
    for s, v in waits:
        if not (isinstance(v, int) and v <= 0):
            eng.wait_ge(s, v)


def wait_alone(eng, settled, *waits):
    waits = [(s, v if isinstance(v, int) else eng.to_reg(v)) for s, v in waits]
    eng.wait_ge(settled, 1)
    since(eng, *waits)


def product(pe, acc, pairs, first=True, final=True):
    for n, (w, m) in enumerate(pairs):
        last = pe.matmul(acc, w, m, start=(first and n == 0), stop=(final and n == len(pairs) - 1))
    return last


class Norm:

    def __init__(self, name, sb, sem, scope, resid, ident, minus_half, settled, turned_ps, slots):
        self.resid, self.ident, self.minus_half, self.settled = resid, ident, minus_half, settled
        self.turned_ps = turned_ps
        self.stats = sb(f"{name}_st", [P, 2, 6], F32, scope)
        self.mv = sb(f"{name}_mv", [P, 2], F32, scope)
        self.ve = sb(f"{name}_ve", [P, 1], F32, scope)
        self.rstd = sb(f"{name}_rs", [P, 1], F32, scope)
        self.xn = sb(f"{name}_xn", [P, D], F32, scope)
        self.hi = [sb(f"{name}_hi{s}", [P, D], F16, scope) for s in range(slots)]
        self.lo = [sb(f"{name}_lo{s}", [P, D], F16, scope) for s in range(slots)]
        (self.part_stats, self.stats_ready, self.eps_added, self.rstd_ready, self.normed, self.turned,
         self.hi_ready, self.lo_ready) = (sem(f"{name}_{n}") for n in (
             "part", "stats", "eps", "rstd", "normed", "turned", "hi", "lo"))

    def vector_stats(self, dve, t, updated=None):
        if updated is not None:
            wait_alone(dve, self.settled, updated)
        for k in range(2):
            last = dve.bn_stats(self.stats[:, k, :], self.resid[:, t, k * HALF:(k + 1) * HALF])
        last.then_inc(self.part_stats, 1)
        wait_alone(dve, self.settled, (self.part_stats, t + 1))
        dve.bn_aggr(self.mv[:, :], self.stats[:, :, :]).then_inc(self.stats_ready, 1)

    def pool_rstd(self, pool, t):
        wait_alone(pool, self.settled, (self.stats_ready, t + 1), (self.normed, t))
        pool.tensor_scalar(self.ve[:, :], self.mv[:, 1:2], EPS_LN, None, ALU.add).then_inc(self.eps_added, 1)
        pool.wait_ge(self.eps_added, t + 1)
        pool.tensor_tensor(self.rstd[:, :], self.ve[:, :], self.minus_half[:, 0:1], ALU.pow).then_inc(self.rstd_ready, 1)

    def vector_norm(self, dve, t):
        since(dve, (self.stats_ready, t + 1), (self.rstd_ready, t + 1), (self.turned, t))
        dve.tensor_scalar(self.xn[:, :], self.resid[:, t, :], self.mv[:, 0:1], self.rstd[:, :],
                          ALU.subtract, ALU.mult).then_inc(self.normed, 1)

    def tensor_turn(self, pe, t, *area_free):
        since(pe, (self.normed, t + 1), *area_free)
        for c in range(DC):
            last = pe.transpose(self.turned_ps[:, c * P:(c + 1) * P], self.xn[:, c * P:(c + 1) * P], self.ident[:, :])
        last.then_inc(self.turned, 1)

    def scalar_hi(self, act, t, s, used):
        since(act, (self.turned, t + 1), used)
        act.activation(self.hi[s][:, :], self.turned_ps[:, :], ACT.Copy).then_inc(self.hi_ready, 1)

    def vector_lo(self, dve, t, s):
        dve.wait_ge(self.hi_ready, t + 1)
        dve.tensor_tensor(self.lo[s][:, :], self.turned_ps[:, :], self.hi[s][:, :], ALU.subtract).then_inc(self.lo_ready, 1)

    def pairs(self, s, hi, lo, chunks=range(DC)):
        out = []
        for c in chunks:
            x_hi, x_lo = self.hi[s][:, c * P:(c + 1) * P], self.lo[s][:, c * P:(c + 1) * P]
            out += [(x_hi, hi(c)), (x_hi, lo(c)), (x_lo, hi(c))]
        return out


def upto(v):
    return min(v, NT) if isinstance(v, int) else v


def phase_stream(nc, sb, ps, sem, sems, env):
    resid, ident, ctx_in, W_base = (env[k] for k in ("resid", "ident", "ctx_in", "W_base"))
    base_hi, base_lo, bias_bc = env["base_hi"], env["base_lo"], env["bias_bc"]
    down_hi, down_lo, up_hi, up_lo = (env[k] for k in ("down_hi", "down_lo", "up_hi", "up_lo"))
    mask, mean_x, rstd_x, coef, dcoef, x = (env[k] for k in ("mask", "mean_x", "rstd_x", "coef", "dcoef", "x"))
    settled = env["const_ready"]
    out = env["out"].rearrange("b (h p) d -> (b h) p d", p=P)
    scope = ExitStack()
    with scope:
        turned_ps = ps("turned_ps", [P, D], scope)
        l_small = ps("l_small", [P, HALF], scope)
        f_small = ps("f_small", [P, HALF], scope)
        q_small = ps("q_small", [P, HALF], scope)
        bank = [ps(f"bank{i}", [P, HALF], scope) for i in range(3)]
        F0, L0, L1, F1, Q0, Q1 = (bank[i % 3] for i in range(6))

        def norm(name, slots):
            return Norm(name, sb, sem, scope, resid, ident, env["minus_half"], settled, turned_ps, slots)

        gate = sb("gate", [P, DC, P], F32, scope)
        prod = sb("prod", [P, D], F32, scope)
        x_loaded = sems("r_x_loaded")
        gate_ready, gate_turned, multiplied, x_added = (
            sem(n) for n in ("gate_ready", "gate_turned", "multiplied", "x_added"))
        nl, nq, nf = norm("nl", 1), norm("nq", 1), norm("nf", 2)
        l_logit, l_e, l_score = (sb(f"l_{n}", [P, H], F32, scope) for n in ("logit", "e", "score"))
        f_e, f_m8, f_rest, f_kept, f_comb = (sb(f"f_{n}", [P, H], F32, scope) for n in ("e", "m8", "rest", "kept", "comb"))
        l_nmax, l_tot, l_inv, q_nmax, q_tot, q_inv, f_nmax, f_den, f_inv = (
            sb(n, [P, 1], F32, scope) for n in ("l_nmax", "l_tot", "l_inv", "q_nmax", "q_tot", "q_inv",
                                                "f_nmax", "f_den", "f_inv"))
        l_low, f_low = (sb(n, [P, HR], F32, scope) for n in ("l_low", "f_low"))
        l_low_hi, l_low_lo, f_low_hi, f_low_lo = (
            sb(n, [P, HR], F16, scope) for n in ("l_low_hi", "l_low_lo", "f_low_hi", "f_low_lo"))
        q_e = sb("q_e", [P, C], F32, scope)
        e_hi, e_lo = (sb(n, [P, C], F16, scope) for n in ("e_hi", "e_lo"))
        c_in = [sb(f"q_c_in{h}", [P, D], F32, scope) for h in range(CH)]
        part = sb("ctx_parts", [P, 4, CH * D], F16, scope)
        v_hi, v_lo = (part[:, k, :].rearrange("p (h d) -> p h d", h=CH) for k in (0, 1))
        k_hi, k_lo = (part[:, k, :].rearrange("p (c n) -> p c n", c=DC) for k in (2, 3))

        c_loaded = sems("q_c_loaded")
        k_turned, k_hi_ready, k_lo_ready, v_hi_ready, v_lo_ready = (
            sem(f"{n}") for n in ("k_turned", "k_hi_ready", "k_lo_ready", "v_hi_ready", "v_lo_ready"))
        l_projected, l_max, l_exp, l_scaled, l_turned, l_hi, l_lo = (
            sem(f"l_{n}") for n in ("projected", "max", "exp", "scaled", "turned", "hi", "lo"))
        f_projected, f_max, f_exp, f_scaled, f_turned, f_hi, f_lo, f_biased, f_stored = (
            sem(f"f_{n}") for n in ("projected", "max", "exp", "scaled", "turned", "hi", "lo", "biased", "stored"))
        q_scored, q_max, q_exp, q_inverse, q_turned, q_hi, q_lo = (
            sem(f"q_{n}") for n in ("scored", "max", "exp", "inverse", "turned", "hi", "lo"))
        l_full, l_added, q_full, q_added, f_full, f_added = (
            sem(n) for n in ("l_full", "l_added", "q_full", "q_added", "f_full", "f_added"))
        l_chain, f_chain = sem("l_chain"), sem("f_chain")
        L_LINKS, F_LINKS = 3, 9

        def steps(eng, step):
            for n in range(4):
                step(n // 2, n % 2, n)
            with eng.Fori(2, NT // 2 - 2) as g:
                for s in range(2):
                    step(g, s, 2 * g + s)
            for n in range(NT - 4, NT + 3):
                step(n // 2, n % 2, n)

        def of_three_on(g, s, n):
            return n + 3, g + 1 + s, 1 - s

        def there(t):
            return not isinstance(t, int) or 0 <= t < NT

        b_in = [sb(f"b_in{s}", [P, D], F32, scope) for s in range(2)]
        b_ps = (F0, f_small)
        b_loaded = sems("b_loaded")
        b_turned, b_hi, b_lo = (sem(f"b_{n}") for n in ("turned", "hi", "lo"))

        def base_block(n, place):
            o = 2 * n + 2 + place
            return (o,) if isinstance(o, int) and o < DC else ()

        def base_part(part, o, half):
            return part[:, 4 * half:4 * half + 4, o * P:(o + 1) * P]

        block = scope.enter_context(nc.Block())

        @block.sync
        def _(sp):
            def load_base(o):
                since(sp, (b_turned, o - 1))
                sp.dma_start(b_in[o % 2][:, :], W_base[o * P:(o + 1) * P, :]).then_inc(b_loaded[o % 2], 16)

            def load_x(t, batch, half):
                sp.wait_ge(x_loaded[half], 16 * batch)
                sp.dma_start(resid[:, t, :], x[batch, half * P:(half + 1) * P, :]).then_inc(x_loaded[half], 16)

            def step(g, s, n):
                if there(n + 4):
                    load_x(n + 4, g + 2, s)
                for place in range(2):
                    for o in base_block(n, place):
                        load_base(o)
                if s == 1 and there(n + 1):
                    for h in range(CH):
                        since(sp, (k_turned, 2 * g + h + 1), (v_hi_ready, 2 * g + h + 1), (v_lo_ready, 2 * g + h + 1))
                        sp.dma_start(c_in[h][:, :], ctx_in[g + 1, h * P:(h + 1) * P, :]).then_inc(c_loaded[h], 16)
                if there(n - 3):
                    sp.wait_ge(f_added, 2 * (n - 3) + 2)
                    sp.dma_start(out[n - 3], resid[:, n - 3, :]).then_inc(f_stored, 16)

            for t in range(2):
                load_x(t, 0, t)
                load_base(t)
            for t in range(2, 4):
                load_x(t, 1, t - 2)
            for h in range(CH):
                sp.dma_start(c_in[h][:, :], ctx_in[0, h * P:(h + 1) * P, :]).then_inc(c_loaded[h], 16)
            steps(sp, step)
            sp.wait_ge(f_stored, 16 * NT)

        @block.gpsimd
        def _(pool):
            def step(g, s, n):
                if there(n - 2):
                    nf.pool_rstd(pool, n - 2)
                if s == 1 and there(n):
                    for h in range(CH):
                        wait_alone(pool, settled, (v_hi_ready, 2 * g + h + 1))
                        pool.tensor_tensor(v_lo[:, h, :], c_in[h][:, :], v_hi[:, h, :], ALU.subtract).then_inc(v_lo_ready, 1)
                if there(n - 2):
                    wait_alone(pool, settled, (nf.normed, n - 1))
                    r = resid[:, n - 2, :]
                    pool.tensor_tensor(r, r, bias_bc[:, :], ALU.add).then_inc(f_biased, 1)
                if there(n):
                    nq.pool_rstd(pool, n)
                if there(n + 2):
                    nl.pool_rstd(pool, n + 2)

            nl.pool_rstd(pool, 0)
            nl.pool_rstd(pool, 1)
            steps(pool, step)

        @block.tensor
        def _(pe):
            def project(nx, s, i, small, free, done, t):
                since(pe, (nx.lo_ready, t + 1), free)
                product(pe, small[:, 0:WA], nx.pairs(s, lambda c: down_hi[i][:, c, :], lambda c: down_lo[i][:, c, :])
                        ).then_inc(done, 1)

            def rise(i, acc, cols, low_hi, low_lo, first):
                return product(pe, acc[:, :], [(low_hi[:, :], up_hi[i][:, cols]), (low_hi[:, :], up_lo[i][:, cols]),
                                               (low_lo[:, :], up_hi[i][:, cols])], first)

            def base(s, acc, cols, chunks):
                product(pe, acc[:, :], nf.pairs(s, lambda c: base_hi[:, c, cols], lambda c: base_lo[:, c, cols], chunks),
                        0 in chunks, False)

            def turn_keys(g, h, *free):
                since(pe, (c_loaded[h], 16 * g + 16), *free)
                for c in range(DC):
                    last = pe.transpose(turned_ps[:, c * P:(c + 1) * P], c_in[h][:, c * P:(c + 1) * P], ident[:, :])
                last.then_inc(k_turned, 1)

            def turn_gate(t, *free):
                since(pe, (gate_ready, t + 1), *free)
                for c in range(DC):
                    last = pe.transpose(turned_ps[:, c * P:(c + 1) * P], gate[:, c, :], ident[:, :])
                last.then_inc(gate_turned, 1)

            def turn_base(o):
                pe.wait_ge(b_loaded[o % 2], 16 * (o // 2) + 16)
                pe.wait_ge(b_lo, o)
                for c in range(DC):
                    last = pe.transpose(b_ps[c // 4][:, (c % 4) * P:(c % 4 + 1) * P], b_in[o % 2][:, c * P:(c + 1) * P],
                                        ident[:, :])
                last.then_inc(b_turned, 1)

            def step(g, s, n):
                m, k, fs = n - 1, n - 3, (s + 1) % 2
                L, Q, F = there(n), there(m), there(k)
                left, right = slice(0, HALF), slice(HALF, D)
                if F and isinstance(k, int) and k == 0:
                    pe.wait_ge(b_lo, DC)
                if F:
                    project(nf, fs, 1, f_small, (f_lo, k), f_projected, k)
                if L:
                    project(nl, 0, 0, l_small, (l_lo, n), l_projected, n)
                if there(n + 1):
                    nl.tensor_turn(pe, n + 1, (nq.lo_ready, n))
                for o in base_block(n, 0):
                    turn_base(o)
                if F:
                    since(pe, (f_added, 2 * k))
                    base(fs, F0, left, range(DC))
                if there(n + 3):
                    turn_gate(n + 3, (nl.lo_ready, n + 2))
                if F:
                    pe.wait_ge(f_scaled, k + 1)
                    pe.transpose(f_small[:, 256:256 + P], f_low[:, :], ident[:, :]).then_inc(f_turned, 1)
                if L:
                    pe.wait_ge(l_scaled, n + 1)
                    pe.transpose(l_small[:, 256:256 + P], l_low[:, :], ident[:, :]).then_inc(l_turned, 1)
                if Q:
                    since(pe, (nq.lo_ready, m + 1), (k_lo_ready, 2 * (g if s else g - 1) + 2), (q_lo, m))
                    product(pe, q_small[:, 0:C], nq.pairs(0, lambda c: k_hi[:, c, :], lambda c: k_lo[:, c, :])
                            ).then_inc(q_scored, 1)
                for o in base_block(n, 1):
                    turn_base(o)
                if F:
                    pe.wait_ge(f_lo, k + 1)
                    rise(1, F0, left, f_low_hi, f_low_lo, False).then_inc(f_full, 1)
                if L:
                    since(pe, (l_lo, n + 1), (q_added, 2 * (n - 2) + 1))
                    rise(0, L0, left, l_low_hi, l_low_lo, True).then_inc(l_full, 1)
                    since(pe, (q_added, 2 * (n - 2) + 2))
                    rise(0, L1, right, l_low_hi, l_low_lo, True).then_inc(l_full, 1)
                if there(n - 2):
                    nf.tensor_turn(pe, n - 2, (multiplied, upto(n + 4)), (nl.lo_ready, upto(n + 2)), (nq.lo_ready, upto(n)))
                if F:
                    pe.wait_ge(f_added, 2 * k + 1)
                    base(fs, F1, right, range(DC // 2))
                if Q:
                    pe.wait_ge(q_exp, m + 1)
                    for j in range(CH):
                        last = pe.transpose(q_small[:, C + j * P:C + (j + 1) * P], q_e[:, j * P:(j + 1) * P], ident[:, :])
                    last.then_inc(q_turned, 1)
                if s == 0 and there(n):
                    turn_keys(g, 0, (nf.lo_ready, n - 1), (multiplied, upto(n + 4)), (nl.lo_ready, upto(n + 2)))
                if F:
                    base(fs, F1, right, range(DC // 2, DC))
                    rise(1, F1, right, f_low_hi, f_low_lo, False).then_inc(f_full, 1)
                if s == 0 and there(n):
                    turn_keys(g, 1, (k_lo_ready, 2 * g + 1))
                if Q:
                    since(pe, (q_lo, m + 1), (v_lo_ready, 2 * (g if s else g - 1) + 2))
                    for i, (acc, cols) in enumerate(((Q0, left), (Q1, right))):
                        since(pe, (l_added, 2 * n + i + 1 if L else 0), (q_added, 2 * m - 1 + i))
                        pairs = []
                        for j in range(CH):
                            h, l = e_hi[:, j * P:(j + 1) * P], e_lo[:, j * P:(j + 1) * P]
                            pairs += [(h, v_hi[:, j, cols]), (h, v_lo[:, j, cols]), (l, v_hi[:, j, cols])]
                        product(pe, acc[:, :], pairs).then_inc(q_full, 1)
                if there(n):
                    nq.tensor_turn(pe, n, *([(k_lo_ready, 2 * g + 2)] if s == 0 else
                                            [(nf.lo_ready, n - 1), (multiplied, upto(n + 4)),
                                             (nl.lo_ready, upto(n + 2))]))

            turn_gate(0)
            turn_base(0)
            turn_gate(1, (multiplied, 1))
            nl.tensor_turn(pe, 0, (multiplied, 2))
            turn_base(1)
            turn_gate(2, (nl.lo_ready, 1))
            steps(pe, step)

        @block.scalar
        def _(act):
            def keys(g, h):
                since(act, (k_turned, 2 * g + h + 1), (q_scored, 2 * g))
                act.activation(k_hi[:, :, h * P:(h + 1) * P], turned_ps[:, :].rearrange("p (c n) -> p c n", c=DC),
                               ACT.Copy).then_inc(k_hi_ready, 1)

            def gates(t, batch, half):
                since(act, (gate_turned, t))
                for c in range(DC):
                    n = batch * DC + c
                    last = act.activation(gate[:, c, :], mask[:, batch, c, half * P:(half + 1) * P], ACT.Identity,
                                          bias=coef[:, 1, bass.ds(n, 1)], scale=dcoef[:, bass.ds(n, 1)])
                last.then_inc(gate_ready, 1)

            def base_hi_part(o):
                act.wait_ge(b_turned, o + 1)
                for half in range(2):
                    last = act.activation(base_part(base_hi, o, half), b_ps[half][:, :].rearrange("p (c n) -> p c n", c=4),
                                          ACT.Copy, scale=WS)
                last.then_inc(b_hi, 1)

            def step(g, s, n):
                m, k, fs = n - 1, n - 3, (s + 1) % 2
                L, Q, F = there(n), there(m), there(k)
                if s == 1 and L:
                    for h in range(CH):
                        since(act, (c_loaded[h], 16 * g + 16), (q_full, 4 * g))
                        act.activation(v_hi[:, h, :], c_in[h][:, :], ACT.Copy).then_inc(v_hi_ready, 1)
                if F:
                    act.wait_ge(f_max, k + 1)
                    act.activation(f_e[:, :], f_small[:, HR:WA], ACT.Exp, bias=f_nmax[:, :],
                                   scale=1.0 / WS).then_inc(f_exp, 1)
                if L:
                    act.wait_ge(l_max, n + 1)
                    act.activation(l_e[:, :], l_logit[:, :], ACT.Exp, bias=l_nmax[:, :],
                                   accum_out=l_tot[:, :]).then_inc(l_exp, 1)
                if there(n + 1):
                    nl.scalar_hi(act, n + 1, 0, (l_projected, n + 1))
                for o in base_block(n, 0):
                    base_hi_part(o)
                if F:
                    since(act, (f_turned, k + 1), (f_full, 2 * k))
                    act.activation(f_low_hi[:, :], f_small[:, 256:256 + P], ACT.Copy).then_inc(f_hi, 1)
                if L:
                    since(act, (l_turned, n + 1), (l_full, 2 * n))
                    act.activation(l_low_hi[:, :], l_small[:, 256:256 + P], ACT.Copy).then_inc(l_hi, 1)
                if Q:
                    since(act, (q_max, m + 1), (q_turned, m))
                    act.activation(q_e[:, :], q_small[:, 0:C], ACT.Exp, bias=q_nmax[:, :],
                                   accum_out=q_tot[:, :]).then_inc(q_exp, 1)
                for o in base_block(n, 1):
                    base_hi_part(o)
                if there(n - 2):
                    nf.scalar_hi(act, n - 2, s, (f_full, 2 * (n - 4) + 2))
                if there(n + 4):
                    gates(n + 4, g + 2, s)
                if Q:
                    since(act, (q_turned, m + 1), (q_full, 2 * m))
                    act.activation(e_hi[:, :], q_small[:, C:2 * C], ACT.Copy).then_inc(q_hi, 1)
                if s == 0 and L:
                    keys(g, 0)
                if s == 0 and L:
                    keys(g, 1)
                if L:
                    nq.scalar_hi(act, n, 0, (q_scored, n))

            for t in range(4):
                if t == 3:
                    nl.scalar_hi(act, 0, 0, (l_projected, 0))
                    base_hi_part(1)
                gates(t, t // 2, t % 2)
                if t == 0:
                    base_hi_part(0)
            steps(act, step)

        @block.vector
        def _(dve):
            def add(t, half, acc, scale, full, added):
                dve.wait_ge(full, 2 * t + half + 1)
                r = resid[:, t, half * HALF:(half + 1) * HALF]
                dve.scalar_tensor_tensor(r, acc[:, :], scale, r, ALU.mult, ALU.add).then_inc(added, 1)

            def gates(n, k, L, F):
                link = {"L": 0, "F": 0}

                def f_link(ins):
                    link["F"] += 1
                    ins.then_inc(f_chain, 1)

                def f_linked():
                    wait_alone(dve, settled, (f_chain, F_LINKS * k + link["F"]))

                def l_link(ins):
                    link["L"] += 1
                    ins.then_inc(l_chain, 1)

                def l_linked():
                    dve.wait_ge(l_chain, L_LINKS * n + link["L"])

                if F:
                    dve.wait_ge(f_projected, k + 1)
                    f_link(dve.tensor_reduce(f_nmax[:, :], f_small[:, HR:WA], AX_X, ALU.max, negate=True))
                if L:
                    dve.wait_ge(l_projected, n + 1)
                    l_link(dve.scalar_tensor_tensor(l_logit[:, :], l_small[:, HR:WA], 1.0 / WS, env["br_bc"][:, :],
                                                    ALU.mult, ALU.add))
                if F:
                    f_linked()
                    dve.tensor_scalar(f_nmax[:, :], f_nmax[:, :], 1.0 / WS, None, ALU.mult).then_inc(f_max, 1)
                if L:
                    l_linked()
                    dve.tensor_reduce(l_nmax[:, :], l_logit[:, :], AX_X, ALU.max, negate=True).then_inc(l_max, 1)
                if F:
                    wait_alone(dve, settled, (f_exp, k + 1))
                    f_link(dve.max(f_m8[:, :], f_e[:, :]))
                if L:
                    dve.wait_ge(l_exp, n + 1)
                    l_link(dve.reciprocal(l_inv[:, :], l_tot[:, :]))
                if F:
                    f_linked()
                    f_link(dve.tensor_tensor(f_den[:, :], f_m8[:, 0:1], f_m8[:, 1:2], ALU.add))
                if L:
                    l_linked()
                    l_link(dve.tensor_scalar(l_score[:, :], l_e[:, :], l_inv[:, :], LORA * H / WS, ALU.mult, ALU.mult))
                if F:
                    f_linked()
                    f_link(dve.memset(f_m8[:, 2:H], -5.0))
                if L:
                    l_linked()
                    dve.tensor_tensor(l_low[:, :].rearrange("p (h r) -> p h r", h=H),
                                      l_small[:, 0:HR].rearrange("p (h r) -> p h r", h=H),
                                      l_score[:, :].unsqueeze(2).broadcast_to([P, H, R]), ALU.mult).then_inc(l_scaled, 1)
                if F:
                    f_linked()
                    f_link(dve.match_replace(f_rest[:, :], f_m8[:, :], f_e[:, :], -1.0))
                    f_link(dve.reciprocal(f_inv[:, :], f_den[:, :]))
                    f_linked()
                    f_link(dve.tensor_tensor(f_kept[:, :], f_rest[:, :], f_e[:, :], ALU.not_equal))
                    f_linked()
                    f_link(dve.tensor_tensor(f_kept[:, :], f_kept[:, :], f_e[:, :], ALU.mult))
                    f_linked()
                    f_link(dve.tensor_scalar(f_comb[:, :], f_kept[:, :], f_inv[:, :], LORA / WS, ALU.mult, ALU.mult))
                    f_linked()
                    assert link["F"] == F_LINKS, link
                    dve.tensor_tensor(f_low[:, :].rearrange("p (h r) -> p h r", h=H),
                                      f_small[:, 0:HR].rearrange("p (h r) -> p h r", h=H),
                                      f_comb[:, :].unsqueeze(2).broadcast_to([P, H, R]), ALU.mult).then_inc(f_scaled, 1)

            def low_part(small, hi, lo, hi_ready, lo_ready, t):
                dve.wait_ge(hi_ready, t + 1)
                dve.tensor_tensor(lo[:, :], small, hi[:, :], ALU.subtract).then_inc(lo_ready, 1)

            def keys(g, h):
                dve.wait_ge(k_hi_ready, 2 * g + h + 1)
                dve.tensor_tensor(k_lo[:, :, h * P:(h + 1) * P], turned_ps[:, :].rearrange("p (c n) -> p c n", c=DC),
                                  k_hi[:, :, h * P:(h + 1) * P], ALU.subtract).then_inc(k_lo_ready, 1)

            def multiply(t, batch, half):
                since(dve, (gate_turned, t + 1), (x_added, t))
                dve.wait_ge(x_loaded[half], 16 * batch + 16)
                dve.scalar_tensor_tensor(prod[:, :], resid[:, t, :], mean_x[:, bass.ds(t, 1)], turned_ps[:, :],
                                         ALU.subtract, ALU.mult).then_inc(multiplied, 1)

            def add_gated(t):
                dve.wait_ge(multiplied, t + 1)
                dve.scalar_tensor_tensor(resid[:, t, :], prod[:, :], rstd_x[:, bass.ds(t, 1)], resid[:, t, :],
                                         ALU.mult, ALU.add).then_inc(x_added, 1)

            def base_lo_part(o):
                dve.wait_ge(b_hi, o + 1)
                for half in range(2):
                    last = dve.scalar_tensor_tensor(base_part(base_lo, o, half),
                                                    b_ps[half][:, :].rearrange("p (c n) -> p c n", c=4), WS,
                                                    base_part(base_hi, o, half), ALU.mult, ALU.subtract)
                last.then_inc(b_lo, 1)

            def step(g, s, n):
                m, k, fs = n - 1, n - 3, (s + 1) % 2
                L, Q, F = there(n), there(m), there(k)
                if there(n - 2):
                    dve.wait_ge(q_inverse, n - 1)
                    for half, acc in ((0, Q0), (1, Q1)):
                        add(n - 2, half, acc, q_inv[:, :], q_full, q_added)
                if there(n - 1):
                    nq.vector_lo(dve, n - 1, 0)
                gates(n, k, L, F)
                if there(n + 1):
                    nl.vector_lo(dve, n + 1, 0)
                for o in base_block(n, 0):
                    base_lo_part(o)
                if there(n - 2):
                    nf.vector_stats(dve, n - 2, (q_added, 2 * (n - 2) + 2))
                if there(n + 3):
                    multiply(*of_three_on(g, s, n))
                if F:
                    low_part(f_small[:, 256:256 + P], f_low_hi, f_low_lo, f_hi, f_lo, k)
                if L:
                    low_part(l_small[:, 256:256 + P], l_low_hi, l_low_lo, l_hi, l_lo, n)
                if there(n - 2):
                    nf.vector_norm(dve, n - 2)
                if Q:
                    dve.wait_ge(q_scored, m + 1)
                    dve.tensor_reduce(q_nmax[:, :], q_small[:, 0:C], AX_X, ALU.max, negate=True).then_inc(q_max, 1)
                for o in base_block(n, 1):
                    base_lo_part(o)
                if F:
                    dve.wait_ge(f_biased, k + 1)
                    add(k, 0, F0, 1.0 / WS, f_full, f_added)
                if L:
                    for half, acc in ((0, L0), (1, L1)):
                        add(n, half, acc, 1.0 / WS, l_full, l_added)
                if there(n + 3):
                    add_gated(n + 3)
                if there(n - 2):
                    nf.vector_lo(dve, n - 2, s)
                if Q:
                    dve.wait_ge(q_exp, m + 1)
                    dve.reciprocal(q_inv[:, :], q_tot[:, :]).then_inc(q_inverse, 1)
                if L:
                    nq.vector_stats(dve, n, (l_added, 2 * n + 2))
                if Q:
                    low_part(q_small[:, C:2 * C], e_hi, e_lo, q_hi, q_lo, m)
                if s == 0 and L:
                    keys(g, 0)
                if there(n + 2):
                    nl.vector_stats(dve, n + 2, (x_added, n + 3))
                if L:
                    nq.vector_norm(dve, n)
                if s == 0 and L:
                    keys(g, 1)
                if there(n + 2):
                    nl.vector_norm(dve, n + 2)
                if F:
                    add(k, 1, F1, 1.0 / WS, f_full, f_added)

            multiply(0, 0, 0)
            add_gated(0)
            nl.vector_stats(dve, 0, (x_added, 1))
            base_lo_part(0)
            multiply(1, 0, 1)
            nl.vector_norm(dve, 0)
            add_gated(1)
            nl.vector_lo(dve, 0, 0)
            base_lo_part(1)
            nl.vector_stats(dve, 1, (x_added, 2))
            multiply(2, 1, 0)
            nl.vector_norm(dve, 1)
            add_gated(2)
            steps(dve, step)


_INS = ["x", "ctx_4096", "L0_xattn_conv_w", "L0_xattn_bn_gamma", "L0_xattn_bn_beta", "L0_ffn_A", "L0_ffn_B",
        "L0_ffn_Wr", "L0_ffn_br", "L1_ffn_W_base", "L1_ffn_b_base", "L1_ffn_W_router", "L1_ffn_A_stack",
        "L1_ffn_B_stack"]


def kernel(**inputs):
    import numpy as _np
    import concourse.bacc as _bacc
    from concourse import mybir as _mybir
    from concourse.bass_utils import run_bass_kernel_spmd as _run

    nc = _bacc.Bacc("TRN2", target_bir_lowering=False, num_devices=1)
    arrays, args = {}, []
    for name in _INS:
        a = _np.ascontiguousarray(inputs[name])
        arrays[f"in_{name}_dram"] = a
        args.append(nc.dram_tensor(f"in_{name}_dram", a.shape, _mybir.dt.from_np(a.dtype), kind="ExternalInput").ap())
    out = nc.dram_tensor("out_0_dram", (B, C, D), F32, kind="ExternalOutput").ap()
    build_kernel(nc, *args, out)
    r = _run(nc, [arrays], core_ids=[0])
    return r.results[0]["out_0_dram"]
```
